# Optimizing a Trainium2 kernel written in Bass

```python
import numpy as np
import jax
import jax.numpy as jnp

def _softmax(x, axis=-1):
    return jax.nn.softmax(x, axis=axis)

def _gelu(x):
    return jax.nn.gelu(x, approximate=True)

def _silu(x):
    return jax.nn.silu(x)

def _sigmoid(x):
    return jax.nn.sigmoid(x)

def _layernorm(x, axis=-1, eps=1e-05):
    m = jnp.mean(x, axis=axis, keepdims=True)
    v = jnp.var(x, axis=axis, keepdims=True)
    return (x - m) / jnp.sqrt(v + eps)

def _scatter_add(tgt, idx, src, axis=0):
    return tgt.at[idx].add(src)

def _segment_sum(src, seg, n):
    return jax.ops.segment_sum(src, seg, n)
kernel_name = 'mk_recurrent_d1_jaxref_r2_365b4e'

def setup_inputs(seed: int=0):
    np.random.seed(seed)
    _w = jnp.asarray

    def _L0_attn_setup():
        import jax, jax.numpy as jnp
        import numpy as np
        BATCH, SEQ, D_MODEL, D_STATE, TIMESCALE = (4, 1024, 512, 64, 2)
        EPS = 1e-06

        def _reference_tuple_inner(x, w_in, b_in, A, Bm, Cm, Dv, w_out, b_out, g_norm):
            B, L, D = x.shape
            S = A.shape[1]
            ts = TIMESCALE
            x_sub = x[:, ::ts] if ts > 1 else x
            x_sub = x_sub * jax.lax.rsqrt(jnp.mean(jnp.square(x_sub), axis=-1, keepdims=True) + EPS) * g_norm
            xz = jnp.einsum('bld,ed->ble', x_sub, w_in) + b_in
            x_proj, gate = jnp.split(xz, 2, axis=-1)
            c_sum = Cm.sum(axis=0)
            h0 = jnp.zeros((B, D, S), dtype=x.dtype)

            def step(h, xt):
                h = jnp.tanh(h * A + xt[:, :, None] * Bm)
                y = h @ c_sum + Dv * xt
                return (h, y)
            h_last, ys = jax.lax.scan(step, h0, jnp.swapaxes(x_proj, 0, 1))
            out = jnp.swapaxes(ys, 0, 1)
            out = out * jax.nn.silu(gate)
            out = jnp.einsum('bld,ed->ble', out, w_out) + b_out
            if ts > 1:
                out = jnp.repeat(out, ts, axis=1)[:, :L]
            return (out, h_last)
        key = jax.random.key(seed)
        ks = jax.random.split(key, 6)
        D, S = (D_MODEL, D_STATE)
        return {'x': jax.random.normal(ks[0], (BATCH, SEQ, D), dtype=jnp.float32), 'w_in': jax.random.normal(ks[1], (2 * D, D), dtype=jnp.float32) * 0.02, 'b_in': jnp.zeros((2 * D,), dtype=jnp.float32), 'A': jax.random.normal(ks[2], (D, S), dtype=jnp.float32) * 0.01, 'Bm': jax.random.normal(ks[3], (D, S), dtype=jnp.float32) * 0.01, 'Cm': jax.random.normal(ks[4], (D, S), dtype=jnp.float32) * 0.01, 'Dv': jnp.ones((D,), dtype=jnp.float32), 'w_out': jax.random.normal(ks[5], (D, D), dtype=jnp.float32) * 0.02, 'b_out': jnp.zeros((D,), dtype=jnp.float32), 'g_norm': jnp.ones((D,), dtype=jnp.float32)}
    _L0_attn_in = _L0_attn_setup()

    def _L0_ffn_setup():
        import jax, jax.numpy as jnp
        import numpy as np
        B, S, D, H, M, E, K = (8, 1024, 512, 1024, 64, 8, 2)
        EH = H // 2

        def _layernorm(x, g, b, eps=1e-05):
            mu = jnp.mean(x, axis=-1, keepdims=True)
            var = jnp.var(x, axis=-1, keepdims=True)
            return (x - mu) * jax.lax.rsqrt(var + eps) * g + b
        key = jax.random.key(seed)
        ks = jax.random.split(key, 16)
        sc = lambda *shape: 1.0 / np.sqrt(shape[0])
        return {'inputs_embeds': jax.random.normal(ks[0], (B, S, D), jnp.float32), 'W_enc': jax.random.normal(ks[1], (D, H), jnp.float32) * sc(D), 'b_enc': jnp.zeros((H,), jnp.float32), 'W_s2c': jax.random.normal(ks[2], (H, M), jnp.float32) * sc(H), 'b_s2c': jnp.zeros((M,), jnp.float32), 'Wr': jax.random.normal(ks[3], (M, E), jnp.float32) * sc(M), 'br': jnp.zeros((E,), jnp.float32), 'W1': jax.random.normal(ks[4], (E, M, EH), jnp.float32) * sc(M), 'b1': jnp.zeros((E, EH), jnp.float32), 'W2': jax.random.normal(ks[5], (E, EH, M), jnp.float32) * sc(EH), 'b2': jnp.zeros((E, M), jnp.float32), 'W_c2s': jax.random.normal(ks[6], (M, H), jnp.float32) * sc(M), 'b_c2s': jnp.zeros((H,), jnp.float32), 'W_dec': jax.random.normal(ks[7], (H, D), jnp.float32) * sc(H), 'b_dec': jnp.zeros((D,), jnp.float32), 'ln_g': jnp.ones((D,), jnp.float32), 'ln_b': jnp.zeros((D,), jnp.float32)}
    _L0_ffn_in = _L0_ffn_setup()
    _d = {'L0_attn_x': _L0_attn_in['x'], 'L0_attn_w_in': _L0_attn_in['w_in'], 'L0_attn_b_in': _L0_attn_in['b_in'], 'L0_attn_A': _L0_attn_in['A'], 'L0_attn_Bm': _L0_attn_in['Bm'], 'L0_attn_Cm': _L0_attn_in['Cm'], 'L0_attn_Dv': _L0_attn_in['Dv'], 'L0_attn_w_out': _L0_attn_in['w_out'], 'L0_attn_b_out': _L0_attn_in['b_out'], 'L0_attn_g_norm': _L0_attn_in['g_norm'], 'L0_ffn_W_enc': _L0_ffn_in['W_enc'], 'L0_ffn_b_enc': _L0_ffn_in['b_enc'], 'L0_ffn_W_s2c': _L0_ffn_in['W_s2c'], 'L0_ffn_b_s2c': _L0_ffn_in['b_s2c'], 'L0_ffn_Wr': _L0_ffn_in['Wr'], 'L0_ffn_br': _L0_ffn_in['br'], 'L0_ffn_W1': _L0_ffn_in['W1'], 'L0_ffn_b1': _L0_ffn_in['b1'], 'L0_ffn_W2': _L0_ffn_in['W2'], 'L0_ffn_b2': _L0_ffn_in['b2'], 'L0_ffn_W_c2s': _L0_ffn_in['W_c2s'], 'L0_ffn_b_c2s': _L0_ffn_in['b_c2s'], 'L0_ffn_W_dec': _L0_ffn_in['W_dec'], 'L0_ffn_b_dec': _L0_ffn_in['b_dec'], 'L0_ffn_ln_g': _L0_ffn_in['ln_g'], 'L0_ffn_ln_b': _L0_ffn_in['ln_b']}
    _x0 = _d['L0_attn_x']
    _d['L0_attn_x'] = jax.random.normal(jax.random.fold_in(jax.random.key(seed), 1), (4, 4096, 512), dtype=_x0.dtype)
    del _x0
    return _d

def reference(L0_attn_x, L0_attn_w_in, L0_attn_b_in, L0_attn_A, L0_attn_Bm, L0_attn_Cm, L0_attn_Dv, L0_attn_w_out, L0_attn_b_out, L0_attn_g_norm, L0_ffn_W_enc, L0_ffn_b_enc, L0_ffn_W_s2c, L0_ffn_b_s2c, L0_ffn_Wr, L0_ffn_br, L0_ffn_W1, L0_ffn_b1, L0_ffn_W2, L0_ffn_b2, L0_ffn_W_c2s, L0_ffn_b_c2s, L0_ffn_W_dec, L0_ffn_b_dec, L0_ffn_ln_g, L0_ffn_ln_b):

    def _L0_attn_ref(x, w_in, b_in, A, Bm, Cm, Dv, w_out, b_out, g_norm):
        import jax, jax.numpy as jnp
        import numpy as np
        BATCH, SEQ, D_MODEL, D_STATE, TIMESCALE = (4, 1024, 512, 64, 2)
        EPS = 1e-06

        def _reference_tuple_inner(x, w_in, b_in, A, Bm, Cm, Dv, w_out, b_out, g_norm):
            B, L, D = x.shape
            S = A.shape[1]
            ts = TIMESCALE
            x_sub = x[:, ::ts] if ts > 1 else x
            x_sub = x_sub * jax.lax.rsqrt(jnp.mean(jnp.square(x_sub), axis=-1, keepdims=True) + EPS) * g_norm
            xz = jnp.einsum('bld,ed->ble', x_sub, w_in) + b_in
            x_proj, gate = jnp.split(xz, 2, axis=-1)
            c_sum = Cm.sum(axis=0)
            h0 = jnp.zeros((B, D, S), dtype=x.dtype)

            def step(h, xt):
                h = jnp.tanh(h * A + xt[:, :, None] * Bm)
                y = h @ c_sum + Dv * xt
                return (h, y)
            h_last, ys = jax.lax.scan(step, h0, jnp.swapaxes(x_proj, 0, 1))
            out = jnp.swapaxes(ys, 0, 1)
            out = out * jax.nn.silu(gate)
            out = jnp.einsum('bld,ed->ble', out, w_out) + b_out
            if ts > 1:
                out = jnp.repeat(out, ts, axis=1)[:, :L]
            return (out, h_last)
        return _reference_tuple_inner(x, w_in, b_in, A, Bm, Cm, Dv, w_out, b_out, g_norm)[0]

    def _L0_ffn_ref(inputs_embeds, W_enc, b_enc, W_s2c, b_s2c, Wr, br, W1, b1, W2, b2, W_c2s, b_c2s, W_dec, b_dec, ln_g, ln_b):
        import jax, jax.numpy as jnp
        import numpy as np
        B, S, D, H, M, E, K = (8, 1024, 512, 1024, 64, 8, 2)
        EH = H // 2

        def _layernorm(x, g, b, eps=1e-05):
            mu = jnp.mean(x, axis=-1, keepdims=True)
            var = jnp.var(x, axis=-1, keepdims=True)
            return (x - mu) * jax.lax.rsqrt(var + eps) * g + b
        b, s, d = inputs_embeds.shape
        spikes_enc = jax.nn.sigmoid(inputs_embeds @ W_enc + b_enc)
        flat = spikes_enc.reshape(b * s, -1)
        cont = flat @ W_s2c + b_s2c
        probs = jax.nn.softmax(cont @ Wr + br, axis=-1)
        topk_w, topk_idx = jax.lax.top_k(probs, K)
        topk_w = topk_w / jnp.sum(topk_w, axis=-1, keepdims=True)
        gate = jnp.sum(jax.nn.one_hot(topk_idx, E, dtype=cont.dtype) * topk_w[..., None], axis=1)
        h = jax.nn.relu(jnp.einsum('tm,emh->eth', cont, W1) + b1[:, None, :])
        y = jnp.einsum('eth,ehm->etm', h, W2) + b2[:, None, :]
        expert_out = jnp.einsum('etm,te->tm', y, gate)
        spikes_moe = jax.nn.sigmoid(expert_out @ W_c2s + b_c2s)
        spikes_moe = spikes_moe.reshape(b, s, -1)
        decoded = spikes_moe @ W_dec + b_dec
        return _layernorm(decoded, ln_g, ln_b)
    x = L0_attn_x
    xn = _layernorm(x, axis=-1)
    s = _L0_attn_ref(xn, L0_attn_w_in, L0_attn_b_in, L0_attn_A, L0_attn_Bm, L0_attn_Cm, L0_attn_Dv, L0_attn_w_out, L0_attn_b_out, L0_attn_g_norm)
    g = _silu(_L0_ffn_ref(xn, L0_ffn_W_enc, L0_ffn_b_enc, L0_ffn_W_s2c, L0_ffn_b_s2c, L0_ffn_Wr, L0_ffn_br, L0_ffn_W1, L0_ffn_b1, L0_ffn_W2, L0_ffn_b2, L0_ffn_W_c2s, L0_ffn_b_c2s, L0_ffn_W_dec, L0_ffn_b_dec, L0_ffn_ln_g, L0_ffn_ln_b))
    x = x + s * g
    return x

_drawn_inputs = setup_inputs


def setup_inputs(seed=0):
    import zlib

    import numpy as np

    out = dict(_drawn_inputs(seed))
    spreads = {'L0_attn_b_in': (0.0, 0.69),
     'L0_attn_Dv': (1.0, 0.6),
     'L0_attn_b_out': (0.0, 0.1),
     'L0_attn_g_norm': (1.0, 0.6),
     'L0_ffn_b_enc': (0.0, 0.8),
     'L0_ffn_b_s2c': (0.0, 0.8),
     'L0_ffn_br': (0.0, 0.8),
     'L0_ffn_b1': (0.0, 0.8),
     'L0_ffn_b2': (0.0, 2.0),
     'L0_ffn_b_c2s': (0.0, 2.0),
     'L0_ffn_b_dec': (0.0, 0.532),
     'L0_ffn_ln_g': (1.0, 0.6),
     'L0_ffn_ln_b': (0.0, 0.8)}
    factors = {'L0_attn_A': 24.041,
     'L0_attn_Bm': 8.0,
     'L0_attn_Cm': 8.0,
     'L0_ffn_W_enc': 8.0,
     'L0_ffn_W_s2c': 7.544,
     'L0_ffn_Wr': 8.0,
     'L0_ffn_W1': 8.0,
     'L0_ffn_W2': 8.0,
     'L0_ffn_W_c2s': 8.0}
    for name, (base, spread) in spreads.items():
        noise = np.random.default_rng([zlib.crc32(name.encode()), seed]).standard_normal(out[name].shape)
        drawn = base * np.exp(spread * noise) if base else spread * noise
        out[name] = jnp.asarray(drawn.astype(out[name].dtype))
    for name, factor in factors.items():
        out[name] = (out[name] * factor).astype(out[name].dtype)
    return out
```

```python
from contextlib import ExitStack

import numpy as np

import concourse.bass as bass
from concourse import mybir

F32 = mybir.dt.float32
ALU = mybir.AluOpType
ACT = mybir.ActivationFunctionType
AX = mybir.AxisListType

P = 128
B = 4
D = 512
S = 64
SP = 32
F = S // SP
STEPS = 32
QUAD = 4
NQ = STEPS // QUAD
CK = 4
RING = 8
KD = D // P
H = 1024
KH = H // P
M = 64
MA = M + 1
E = 8
EH = 512
T2 = 2 * P
NFILL = 38
LN_EPS = 1e-5
RMS_EPS = 1e-6

FILL_ENC, FILL_FIN, FILL_CONT, FILL_GATE, FILL_CONTE = 0, 4, 6, 7, 8
FILL_W1 = list(range(12, 20)) + list(range(22, 26)) + list(range(28, 32))
FILL_XT, FILL_WIN, FILL_C2S, FILL_DEC = 20, 26, 32, 36


def build(nc, x, w_inT, b_in, A_T, B_T, Cm, Dv, w_outT, b_out, g_norm, W_enc, b_enc, W_s2c, b_s2c,
          Wr, br, W1, b1, W2, b2, W_c2s, b_c2s, W_dec, b_dec, ln_g, ln_b, out):
    NB = x.shape[1] // (2 * STEPS)
    LAST = NB - 1
    LT = NB * STEPS

    x_rows = x.rearrange("b (i m j q) d -> i j m b (q d)", m=NQ, j=QUAD, q=2)
    out_rows = out.rearrange("b (i m j q) d -> i j m b (q d)", m=NQ, j=QUAD, q=2)
    scratch = nc.dram_tensor("x_proj_scratch", (B, LT, D), F32, kind="Internal").ap()
    scratch_rows = scratch.rearrange("b (i m j) d -> i j m b d", m=NQ, j=QUAD)
    scratch_chunk = scratch.rearrange("b (i c t) d -> i c b (t d)", c=STEPS // CK, t=CK)

    with ExitStack() as ctx:
        def sb(name, shape):
            return ctx.enter_context(nc.sbuf_tensor(name, shape, F32))

        def pb(name, shape):
            return ctx.enter_context(nc.psum_tensor(name, shape, F32))

        def sem(name):
            return ctx.enter_context(nc.semaphore(name))

        w_in = sb("w_in", [P, KD, 2 * D])
        w_out = sb("w_out", [P, KD, D])
        w_enc = sb("w_enc", [P, KD, H])
        w_s2c = sb("w_s2c", [P, KH, MA])
        w_r = sb("w_r", [MA, E])
        w_1 = sb("w_1", [MA, E, EH])
        w_2 = sb("w_2", [P, E * EH // P, M])
        bias_2 = sb("bias_2", [E, M])
        w_c2s = sb("w_c2s", [P, H])
        w_dec = sb("w_dec", [P, KH, D])
        bt = sb("bt", [P, F, D])
        bias_rows = sb("bias_rows", [P, D])
        ones = sb("ones", [P, P])
        b_in_all = sb("b_in_all", [P, 2 * D])
        ln_g_all = sb("ln_g_all", [P, D])
        ln_b_all = sb("ln_b_all", [P, D])
        dv_all = sb("dv_all", [P, D])
        b_enc_col = sb("b_enc_col", [P, KH])
        b_c2s_col = sb("b_c2s_col", [P, KH])
        g_col = sb("g_col", [P, KD])
        ident = sb("ident", [P, P])
        before = sb("before", [P, E, E])
        c_wide = sb("c_wide", [P, F, 2 * SP - 4])
        minus_half = sb("minus_half", [P, 2])
        minus_one = sb("minus_one", [P, 2])
        ln_eps = sb("ln_eps", [P, 2])
        rms_eps = sb("rms_eps", [P, 2])
        h = sb("h", [P, RING, F, D])
        xb = sb("xb", [P, 2, CK, D])
        u = sb("u", [P, 2, F, D])
        xbuf = sb("xbuf", [P, 2, D])
        xnT = sb("xnT", [P, 2, KD, 2, P])
        xp = sb("xp", [P, 2, D])
        gt = sb("gt", [P, 2, D])
        wide = sb("wide", [P, KH, T2])
        conte = sb("conte", [P, 2, E, MA])
        hT = sb("hT", [P, 2, 2 * T2])
        eoT = sb("eoT", [P, T2])
        cont = sb("cont", [P, 2, MA])
        g = sb("g", [P, 2, D])
        sg = sb("sg", [P, D])
        gateT = sb("gateT", [E, T2])
        logit = sb("logit", [P, 2, E])
        sel = sb("sel", [P, 2, E])
        over = sb("over", [P, 2, E, E])
        top_sum = sb("top_sum", [P, 2])
        gate = sb("gate", [P, 2, E])
        p_st = sb("p_st", [P, 2, 6])
        p_mv = sb("p_mv", [P, 2, 2])
        p_r = sb("p_r", [P, 2])
        p_nm = sb("p_nm", [P, 2])
        p_rr = sb("p_rr", [P, 2])
        d_st = sb("d_st", [P, 2, 6])
        d_mv = sb("d_mv", [P, 2, 2])
        d_r = sb("d_r", [P, 2])
        d_nm = sb("d_nm", [P, 2])
        contT = eoT[0:MA, :]
        conteT = wide[0:MA, :, :].rearrange("p (e) t -> p e t", e=E)
        conte_flat = conte[:, :, :, :].rearrange("p q e m -> p (q e m)")
        o = conte_flat[:, 0:D]
        oT = conte_flat[:, D:2 * D].rearrange("p (k t) -> p k t", k=KD)

        ps_A = pb("ps_A", [P, F, D])
        ps_z = pb("ps_z", [P, F, D])
        ps_y = pb("ps_y", [P, D])
        bank = [pb("bank0", [P, D]), pb("bank1", [P, D])]
        ps_acc = pb("ps_acc", [P, D])
        eo_acc = ps_acc[:, 0:T2]
        cont_acc = ps_acc[:, T2:T2 + 2 * MA].rearrange("p (q m) -> p q m", q=2)
        L0 = T2 + 2 * MA
        logit_acc = ps_acc[:, L0:L0 + 2 * E].rearrange("p (q e) -> p q e", q=2)
        atleast = ps_acc[:, 0:2 * E * E].rearrange("p (q e j) -> p q e j", q=2, e=E)
        rank = ps_acc[:, 128:144].rearrange("p (q e) -> p q e", q=2)
        selected = ps_acc[:, 144:160].rearrange("p (q e) -> p q e", q=2)
        margin = ps_acc[:, 160:176].rearrange("p (q e) -> p q e", q=2)
        weight = ps_acc[:, 176:192].rearrange("p (q e) -> p q e", q=2)

        weights_loaded = sem("weights_loaded")
        consts_made = sem("consts_made")
        pool_made = sem("pool_made")
        c_summed = sem("c_summed")
        ready = sem("ready")
        bank_filled = [sem("bank0_filled"), sem("bank1_filled")]
        bank_drained = [sem("bank0_drained"), sem("bank1_drained")]
        u_ready = sem("u_ready")
        m_done = sem("m_done")
        z_ready = sem("z_ready")
        h_ready = sem("h_ready")
        y_done = sem("y_done")
        stats_settled = sem("stats_settled")
        y_taken = sem("y_taken")
        chunk_loaded = [sem("chunk0_loaded"), sem("chunk1_loaded")]
        x_loaded = sem("x_loaded")
        scratch_stored = sem("scratch_stored")
        out_stored = sem("out_stored")
        p_stats_done = sem("p_stats_done")
        p_scale_steps = sem("p_scale_steps")
        p_normed = sem("p_normed")
        gate_sigmoid = sem("gate_sigmoid")
        sg_used = sem("sg_used")
        cont_ready = sem("cont_ready")
        cont_copied = sem("cont_copied")
        logits_ready = sem("logits_ready")
        logits_copied = sem("logits_copied")
        route_steps = sem("route_steps")
        weight_ready = sem("weight_ready")
        gate_ready = sem("gate_ready")
        conte_ready = sem("conte_ready")
        eo_ready = sem("eo_ready")
        eo_copied = sem("eo_copied")
        d_stats_done = sem("d_stats_done")
        d_scale_steps = sem("d_scale_steps")
        g_normed = sem("g_normed")
        g_sigmoid = sem("g_sigmoid")
        t1_ready = sem("t1_ready")
        o_ready = sem("o_ready")
        g_times_s = sem("g_times_s")
        out_ready = sem("out_ready")

        n_loads = [0]

        def fill_number(blk, k):
            if isinstance(blk, int) and blk == 0:
                return 4 + k - (2 if k >= 6 else 0)
            if isinstance(blk, int) and blk == LAST:
                return NFILL * blk + 2 + k - (2 if k >= 22 else 0) - (2 if k >= 28 else 0)
            return NFILL * blk + 2 + k

        def fill_count(n_or_blk, k):
            if isinstance(n_or_blk, int):
                return fill_number(n_or_blk, k) // 2 + 1
            return (NFILL // 2) * n_or_blk + (2 + k) // 2 + 1

        def proj_fill(blk, k):
            if isinstance(blk, int) and blk == 0:
                return None, (k - FILL_XT if k < FILL_WIN else 2 + k - FILL_WIN)
            return blk - 1, k

        def fin_fill(blk, k):
            if isinstance(blk, int) and blk == LAST:
                return None, NFILL * LAST + 2 + 34 + k - FILL_FIN
            return blk + 1, k

        def count_of(at):
            body, k = at
            return k // 2 + 1 if body is None else fill_count(body, k)

        def wait_filled(eng, at):
            eng.wait_ge(bank_filled[at[1] % 2], count_of(at))

        def wait_drained(eng, at):
            eng.wait_ge(bank_drained[at[1] % 2], count_of(at))

        def wait_free(eng, at):
            if at[0] is None and at[1] < 2:
                return
            eng.wait_ge(bank_drained[at[1] % 2], count_of(at) - 1)

        def filled(ins, at):
            ins.then_inc(bank_filled[at[1] % 2], 1)

        def drained(ins, at):
            ins.then_inc(bank_drained[at[1] % 2], 1)

        def x_load_number(blk, fin):
            if fin:
                return 2 * blk + (1 if is_last(blk) else 2)
            if isinstance(blk, int) and blk == 0:
                return 0
            return 2 * blk - 1

        def sg_number(blk, tile):
            if tile is None:
                return 0 if isinstance(blk, int) and blk == 0 else 3 * blk - 2
            if isinstance(blk, int) and blk == LAST:
                return 3 * blk + 1 + tile
            return 3 * blk + 2 + tile

        block = ctx.enter_context(nc.Block())

        def run_bodies(eng, body):
            body(0, 0)
            with eng.Fori(0, (LAST - 1) // 2) as pair:
                body(2 * pair + 1, 1)
                body(2 * pair + 2, 0)
            body(LAST, LAST % 2)

        def is_first(blk):
            return isinstance(blk, int) and blk == 0

        def is_last(blk):
            return isinstance(blk, int) and blk == LAST

        @block.sync
        def _(sp):
            def load(dst, src):
                sp.dma_start(dst, src).then_inc(weights_loaded, 16)
                n_loads[0] += 1

            def load_x(blk, fin):
                if fin:
                    if not is_last(blk):
                        wait_drained(sp, proj_fill(blk + 1, FILL_XT + 1))
                elif not is_first(blk):
                    if isinstance(blk, int) and blk == 1:
                        wait_drained(sp, proj_fill(0, FILL_XT + 1))
                    else:
                        sp.wait_ge(out_ready, blk - 1)
                for j in range(QUAD):
                    sp.dma_start(xbuf[32 * j:32 * j + 32, :, :].rearrange("p q d -> p (q d)"),
                                 x_rows[blk, j]).then_inc(x_loaded, 16)

            def store_scratch(blk, par):
                wait_drained(sp, proj_fill(blk, FILL_WIN))
                for j in range(QUAD):
                    sp.dma_start(scratch_rows[blk, j], xp[32 * j:32 * j + 32, par, :]
                                 ).then_inc(scratch_stored, 16)

            def load_chunk(blk, c):
                if not (is_first(blk) and c < 2):
                    sp.wait_ge(u_ready, STEPS * blk + CK * (c - 1))
                if c == 0:
                    sp.wait_ge(scratch_stored, 16 * QUAD * (blk + 1))
                for b in range(B):
                    sp.dma_start(xb[SP * b:SP * b + SP, c % 2, :, :].rearrange("p t d -> p (t d)"),
                                 scratch_chunk[blk, c, b].partition_broadcast(SP)
                                 ).then_inc(chunk_loaded[c % 2], 16)

            def store_out(blk):
                sp.wait_ge(out_ready, blk + 1)
                for j in range(QUAD):
                    sp.dma_start(out_rows[blk, j],
                                 g[32 * j:32 * j + 32, :, :].rearrange("p q d -> p (q d)")
                                 ).then_inc(out_stored, 16)

            load_x(0, False)
            load(g_col[:, :], g_norm)
            load(w_in[:, :, :], w_inT.rearrange("(k p) n -> p k n", p=P))
            load(b_in_all[:, :], b_in.partition_broadcast(P))
            for b in range(B):
                load(h[SP * b:SP * b + SP, 0, :, :], A_T.rearrange("(f s) d -> s f d", f=F))
                load(bt[SP * b:SP * b + SP, :, :], B_T.rearrange("(f s) d -> s f d", f=F))
            load(h[:, 1, 0, 0:KD * S].rearrange("p (k s) -> p k s", k=KD), Cm.rearrange("(k p) s -> p k s", p=P))
            load(w_enc[:, :, :], W_enc.rearrange("(k p) n -> p k n", p=P))
            load(b_enc_col[:, :], b_enc)
            load(w_s2c[:, :, 0:M], W_s2c.rearrange("(k p) n -> p k n", p=P))
            load(bias_rows[0:1, :], b_dec.partition_broadcast(1))
            load(bias_rows[32:33, :], b_out.partition_broadcast(1))
            load(bias_rows[64:65, 0:M], b_s2c.partition_broadcast(1))
            load(w_r[0:M, :], Wr)
            load(w_r[M:MA, :], br.partition_broadcast(1))
            load(w_1[0:M, :, :], W1.rearrange("e m h -> m e h"))
            load(w_1[M:MA, :, :].rearrange("p e h -> p (e h)"), b1.rearrange("e h -> (e h)").partition_broadcast(1))
            load(w_2[:, :, :], W2.rearrange("e (t p) m -> p (e t) m", p=P))
            load(bias_2[:, :], b2)
            for half in range(2):
                load(w_c2s[M * half:M * half + M, :], W_c2s)
            load(b_c2s_col[:, :], b_c2s)
            load(w_dec[:, :, :], W_dec.rearrange("(k p) n -> p k n", p=P))
            load(w_out[:, :, :], w_outT.rearrange("(k p) n -> p k n", p=P))
            load(ln_g_all[:, :], ln_g.partition_broadcast(P))
            load(ln_b_all[:, :], ln_b.partition_broadcast(P))
            load(dv_all[:, :], Dv.partition_broadcast(P))

            store_scratch(0, 0)
            load_chunk(0, 0)

            def body(blk, par):
                load_chunk(blk, 1)
                if not is_first(blk):
                    load_x(blk - 1, True)
                load_chunk(blk, 2)
                load_chunk(blk, 3)
                if not is_first(blk):
                    store_out(blk - 1)
                if not is_last(blk):
                    load_x(blk + 1, False)
                load_chunk(blk, 4)
                load_chunk(blk, 5)
                load_chunk(blk, 6)
                if not is_last(blk):
                    store_scratch(blk + 1, 1 - par)
                load_chunk(blk, 7)
                if not is_last(blk):
                    load_chunk(blk + 1, 0)

            run_bodies(sp, body)
            load_x(LAST, True)
            store_out(LAST)
            sp.wait_ge(out_stored, 16 * QUAD * NB)
            sp.wait_ge(scratch_stored, 16 * QUAD * NB)

        ALL_LOADED = 16 * n_loads[0]

        @block.gpsimd
        def _(pool):
            pool.memset(ident[:, :], 0.0).then_inc(pool_made, 1)
            pool.memset(before[:, :, :], 1.0).then_inc(pool_made, 1)
            pool.memset(minus_half[:, :], -0.5).then_inc(pool_made, 1)
            pool.memset(minus_one[:, :], -1.0).then_inc(pool_made, 1)
            pool.memset(ln_eps[:, :], LN_EPS).then_inc(pool_made, 1)
            pool.memset(rms_eps[:, :], RMS_EPS).then_inc(pool_made, 1)
            pool.wait_ge(pool_made, 6)
            pool.affine_select(out=ident[:, :], in_=ident[:, :], compare_op=ALU.not_equal, fill=1.0,
                               base=0, pattern=[[-1, P]], channel_multiplier=1).then_inc(pool_made, 1)
            pool.affine_select(out=before[:, :, :], in_=before[:, :, :], compare_op=ALU.is_ge, fill=0.0,
                               base=-1, pattern=[[1, E], [-1, E]], channel_multiplier=0).then_inc(pool_made, 1)

            def step(blk, tau):
                c = tau // CK
                if tau % CK == 0:
                    pool.wait_ge(chunk_loaded[c % 2], 16 * B * (4 * blk + c // 2 + 1))
                if not (is_first(blk) and tau < 2):
                    pool.wait_ge(z_ready, 2 * STEPS * blk + 2 * tau - 2)
                xt = xb[:, c % 2, tau % CK, :].unsqueeze(1).to_broadcast([P, F, D])
                pool.tensor_tensor(u[:, tau % 2, :, :], xt, bt[:, :, :], ALU.mult).then_inc(u_ready, 1)

            def proj_scale(blk):
                n = [0]

                def link(ins):
                    ins.then_inc(p_scale_steps, 1)
                    n[0] += 1

                def wait_link():
                    pool.wait_ge(p_scale_steps, 8 * blk + n[0])

                pool.wait_ge(p_stats_done, 4 * blk + 4)
                link(pool.tensor_tensor(p_rr[:, :], p_mv[:, :, 1], ln_eps[:, :], ALU.add))
                wait_link()
                link(pool.tensor_tensor(p_r[:, :], p_rr[:, :], minus_half[:, :], ALU.pow))
                wait_link()
                link(pool.tensor_tensor(p_nm[:, :], p_mv[:, :, 0], p_r[:, :], ALU.mult))
                wait_link()
                link(pool.tensor_tensor(p_nm[:, :], p_nm[:, :], minus_one[:, :], ALU.mult))
                link(pool.tensor_tensor(p_rr[:, :], p_mv[:, :, 1], p_r[:, :], ALU.mult))
                wait_link()
                link(pool.tensor_tensor(p_rr[:, :], p_rr[:, :], p_r[:, :], ALU.mult))
                wait_link()
                link(pool.tensor_tensor(p_rr[:, :], p_rr[:, :], rms_eps[:, :], ALU.add))
                wait_link()
                link(pool.tensor_tensor(p_rr[:, :], p_rr[:, :], minus_half[:, :], ALU.pow))

            def gate_mul(blk, par):
                pool.wait_ge(gate_sigmoid, blk + 1)
                pool.tensor_tensor(gt[:, par, :], gt[:, par, :], sg[:, :], ALU.mult).then_inc(sg_used, 1)

            def dec_scale(blk, q):
                t = 2 * blk + q
                pool.wait_ge(d_stats_done, 2 * t + 2)
                r, nm = d_r[:, q:q + 1], d_nm[:, q:q + 1]
                pool.tensor_tensor(r, d_mv[:, q, 1:2], ln_eps[:, 0:1], ALU.add).then_inc(d_scale_steps, 1)
                pool.wait_ge(d_scale_steps, 4 * t + 1)
                pool.tensor_tensor(r, r, minus_half[:, 0:1], ALU.pow).then_inc(d_scale_steps, 1)
                pool.wait_ge(d_scale_steps, 4 * t + 2)
                pool.tensor_tensor(nm, d_mv[:, q, 0:1], r, ALU.mult).then_inc(d_scale_steps, 1)
                pool.wait_ge(d_scale_steps, 4 * t + 3)
                pool.tensor_tensor(nm, nm, minus_one[:, 0:1], ALU.mult).then_inc(d_scale_steps, 1)

            def dec_gain(blk, q):
                wait_drained(pool, (blk, FILL_DEC + q))
                pool.tensor_tensor(g[:, q, :], g[:, q, :], ln_g_all[:, :], ALU.mult).then_inc(g_normed, 1)

            def dec_shift(blk, q):
                pool.wait_ge(g_normed, 2 * (2 * blk + q) + 1)
                pool.tensor_tensor(g[:, q, :], g[:, q, :], ln_b_all[:, :], ALU.add).then_inc(g_normed, 1)

            def dec_silu(blk, q):
                pool.wait_ge(g_sigmoid, 2 * blk + q + 1)
                pool.tensor_tensor(g[:, q, :], g[:, q, :], sg[:, :], ALU.mult).then_inc(sg_used, 1)

            def fin_skip(blk, par):
                pool.tensor_tensor(o, xp[:, par, :], dv_all[:, :], ALU.mult).then_inc(t1_ready, 1)

            def fin_gate(blk, par):
                pool.wait_ge(y_taken, blk + 1)
                pool.tensor_tensor(o, o, gt[:, par, :], ALU.mult).then_inc(o_ready, 1)

            def fin_add(blk, q):
                if q == 0:
                    pool.wait_ge(g_times_s, 2 * blk + 2)
                    pool.wait_ge(x_loaded, 16 * QUAD * (x_load_number(blk, True) + 1))
                ins = pool.tensor_tensor(g[:, q, :], g[:, q, :], xbuf[:, q, :], ALU.add)
                if q == 1:
                    ins.then_inc(out_ready, 1)

            pool.wait_ge(ready, 2)
            proj_scale(0)
            gate_mul(0, 0)

            def body(blk, par):
                for tau in range(STEPS):
                    step(blk, tau)
                    if not is_first(blk):
                        if tau == 0:
                            dec_gain(blk - 1, 0)
                        if tau == 1:
                            dec_scale(blk - 1, 1)
                            dec_shift(blk - 1, 0)
                        if tau == 2:
                            fin_skip(blk - 1, 1 - par)
                        if tau == 3:
                            dec_gain(blk - 1, 1)
                        if tau == 4:
                            fin_gate(blk - 1, 1 - par)
                        if tau == 5:
                            dec_shift(blk - 1, 1)
                        if tau == 6:
                            dec_silu(blk - 1, 0)
                        if tau == 8:
                            dec_silu(blk - 1, 1)
                        if tau == 12:
                            fin_add(blk - 1, 0)
                        if tau == 13:
                            fin_add(blk - 1, 1)
                    if not is_last(blk):
                        if tau == 17:
                            proj_scale(blk + 1)
                        if tau == 27:
                            gate_mul(blk + 1, 1 - par)
                    if tau == 31:
                        dec_scale(blk, 0)

            run_bodies(pool, body)
            lp = LAST % 2
            dec_gain(LAST, 0)
            dec_scale(LAST, 1)
            dec_shift(LAST, 0)
            fin_skip(LAST, lp)
            dec_gain(LAST, 1)
            dec_shift(LAST, 1)
            dec_silu(LAST, 0)
            dec_silu(LAST, 1)
            fin_gate(LAST, lp)
            fin_add(LAST, 0)
            fin_add(LAST, 1)

        @block.scalar
        def _(act):
            def tanh(blk, tau):
                for f in range(F):
                    act.wait_ge(z_ready, 2 * STEPS * blk + 2 * tau + f + 1)
                    if f == 0 and tau % QUAD == 0 and not (is_first(blk) and tau < RING):
                        act.wait_ge(y_done, NQ * blk + tau // QUAD - 1)
                    act.activation(h[:, tau % RING, f, :], ps_z[:, f, :], ACT.Tanh).then_inc(h_ready, 1)

            def proj_norm(blk):
                act.wait_ge(p_scale_steps, 8 * blk + 8)
                for q in range(2):
                    act.activation(xbuf[:, q, :], xbuf[:, q, :], ACT.Identity, bias=p_nm[:, q:q + 1],
                                   scale=p_r[:, q:q + 1]).then_inc(p_normed, 1)

            def proj_evac(blk, par, q):
                at = proj_fill(blk, FILL_XT + q)
                wait_filled(act, at)
                drained(act.activation(xnT[:, par, :, q, :],
                                       bank[q][:, :].rearrange("p (k t) -> p k t", k=KD), ACT.Copy), at)

            def gate_sig(blk, par):
                wait_drained(act, proj_fill(blk, FILL_WIN + 1))
                if not is_first(blk):
                    act.wait_ge(sg_used, sg_number(blk, None))
                act.activation(sg[:, :], gt[:, par, :], ACT.Sigmoid).then_inc(gate_sigmoid, 1)

            def spikes(blk, base, k, bias):
                at = (blk, base + k)
                wait_filled(act, at)
                for half in range(2):
                    m = 2 * k + half
                    ins = act.activation(wide[:, m, :], bank[k % 2][:, T2 * half:T2 * half + T2],
                                         ACT.Sigmoid, bias=bias[:, m:m + 1])
                drained(ins, at)

            def cont_copy(blk):
                act.wait_ge(cont_ready, blk + 1)
                act.activation(cont[:, :, :], cont_acc, ACT.Copy).then_inc(cont_copied, 1)

            def contT_copy(blk):
                at = (blk, FILL_CONT)
                wait_filled(act, at)
                drained(act.activation(contT, bank[0][0:MA, 0:T2], ACT.Copy), at)

            def logits_copy(blk):
                act.wait_ge(logits_ready, blk + 1)
                act.activation(logit[:, :, :], logit_acc, ACT.Copy).then_inc(logits_copied, 1)

            def route_sig(blk):
                act.wait_ge(route_steps, 9 * blk + 8)
                act.activation(weight, margin, ACT.Sigmoid).then_inc(weight_ready, 1)

            def scale_cont(blk):
                act.wait_ge(gate_ready, blk + 1)
                for q in range(2):
                    for e in range(E):
                        ins = act.activation(conte[:, q, e, :], cont_acc[:, q, :], ACT.Copy,
                                             scale=gate[:, q, e:e + 1])
                ins.then_inc(conte_ready, 1)

            def gateT_copy(blk):
                at = (blk, FILL_GATE)
                wait_filled(act, at)
                drained(act.activation(gateT[:, :], bank[1][0:E, 0:T2], ACT.Copy), at)

            def conteT_copy(blk, k):
                at = (blk, FILL_CONTE + k)
                wait_filled(act, at)
                drained(act.activation(conteT[:, 2 * k:2 * k + 2, :],
                                       bank[k % 2][0:MA, :].rearrange("p (e t) -> p e t", e=2), ACT.Copy), at)

            def relu(blk, n):
                at = (blk, FILL_W1[n])
                wait_filled(act, at)
                drained(act.activation(hT[:, n % 2, :], bank[n % 2][:, :], ACT.Relu), at)

            def eo_copy(blk):
                act.wait_ge(eo_ready, blk + 1)
                act.activation(eoT[:, :], eo_acc, ACT.Copy).then_inc(eo_copied, 1)

            def dec_norm(blk, q):
                at = (blk, FILL_DEC + q)
                act.wait_ge(d_scale_steps, 4 * (2 * blk + q) + 4)
                if not is_first(blk):
                    act.wait_ge(out_stored, 16 * QUAD * blk)
                drained(act.activation(g[:, q, :], bank[q][:, :], ACT.Identity, bias=d_nm[:, q:q + 1],
                                       scale=d_r[:, q:q + 1]), at)

            def dec_sig(blk, q):
                act.wait_ge(g_normed, 2 * (2 * blk + q) + 2)
                act.wait_ge(sg_used, sg_number(blk, q))
                act.activation(sg[:, :], g[:, q, :], ACT.Sigmoid).then_inc(g_sigmoid, 1)

            def fin_evac(blk):
                at = fin_fill(blk, FILL_FIN)
                wait_filled(act, at)
                drained(act.activation(oT, bank[0][:, :].rearrange("p (k t) -> p k t", k=KD), ACT.Copy), at)

            act.wait_ge(weights_loaded, ALL_LOADED)
            act.activation(ps_A[:, 0, :], h[:, 0, 0, :], ACT.Copy)
            act.activation(ps_A[:, 1, :], h[:, 0, 1, :], ACT.Copy).then_inc(ready, 1)
            proj_norm(0)
            proj_evac(0, 0, 0)
            proj_evac(0, 0, 1)
            gate_sig(0, 0)

            def body(blk, par):
                for tau in range(STEPS):
                    tanh(blk, tau)
                    if tau == 1:
                        spikes(blk, FILL_ENC, 0, b_enc_col)
                    if tau == 2:
                        if not is_first(blk):
                            dec_norm(blk - 1, 1)
                        spikes(blk, FILL_ENC, 1, b_enc_col)
                    if tau == 3 and not is_first(blk):
                        dec_sig(blk - 1, 0)
                    if tau == 4:
                        spikes(blk, FILL_ENC, 2, b_enc_col)
                    if tau == 5:
                        spikes(blk, FILL_ENC, 3, b_enc_col)
                    if tau == 7 and not is_first(blk):
                        dec_sig(blk - 1, 1)
                    if tau == 8:
                        cont_copy(blk)
                        if not is_first(blk):
                            fin_evac(blk - 1)
                    if tau == 9:
                        contT_copy(blk)
                    if tau == 10:
                        logits_copy(blk)
                    if tau == 13:
                        route_sig(blk)
                    if tau == 14:
                        scale_cont(blk)
                        gateT_copy(blk)
                    if tau == 15:
                        for k in range(4):
                            conteT_copy(blk, k)
                    if tau == 16:
                        relu(blk, 0)
                    if tau == 17:
                        relu(blk, 1)
                        relu(blk, 2)
                    if tau == 18:
                        relu(blk, 3)
                        relu(blk, 4)
                        if not is_last(blk):
                            proj_norm(blk + 1)
                    if tau == 19:
                        relu(blk, 5)
                        relu(blk, 6)
                    if tau == 20:
                        relu(blk, 7)
                        if not is_last(blk):
                            proj_evac(blk + 1, 1 - par, 0)
                            proj_evac(blk + 1, 1 - par, 1)
                    if tau == 21:
                        relu(blk, 8)
                        relu(blk, 9)
                    if tau == 22:
                        relu(blk, 10)
                        relu(blk, 11)
                    if tau == 25:
                        if not is_last(blk):
                            gate_sig(blk + 1, 1 - par)
                        relu(blk, 12)
                        relu(blk, 13)
                    if tau == 26:
                        relu(blk, 14)
                        relu(blk, 15)
                    if tau == 27:
                        eo_copy(blk)
                        spikes(blk, FILL_C2S, 0, b_c2s_col)
                        spikes(blk, FILL_C2S, 1, b_c2s_col)
                    if tau == 28:
                        spikes(blk, FILL_C2S, 2, b_c2s_col)
                        spikes(blk, FILL_C2S, 3, b_c2s_col)
                    if tau == 31:
                        dec_norm(blk, 0)

            run_bodies(act, body)
            dec_norm(LAST, 1)
            dec_sig(LAST, 0)
            dec_sig(LAST, 1)
            fin_evac(LAST)

        @block.tensor
        def _(pe):
            def y(blk, k):
                pe.wait_ge(h_ready, 2 * STEPS * blk + 2 * QUAD * (k + 1))
                if k == 0 and not is_first(blk):
                    pe.wait_ge(y_taken, blk)
                for f in range(F):
                    for j in range(QUAD):
                        ins = pe.matmul(ps_y[32 * j:32 * j + 32, :],
                                        c_wide[:, f, SP - 4 - 4 * k:2 * SP - 4 - 4 * k],
                                        h[:, (QUAD * k + j) % RING, f, :],
                                        start=(k == 0 and f == 0), stop=(k == NQ - 1 and f == F - 1))
                ins.then_inc(y_done, 1)

            def proj_transpose(blk, q):
                at = proj_fill(blk, FILL_XT + q)
                pe.wait_ge(p_normed, 2 * blk + q + 1)
                wait_free(pe, at)
                for k in range(KD):
                    ins = pe.transpose(bank[q][:, P * k:P * k + P], xbuf[:, q, P * k:P * k + P], ident[:, :])
                filled(ins, at)

            def proj_in(blk, par, half):
                at = proj_fill(blk, FILL_WIN + half)
                wait_drained(pe, proj_fill(blk, FILL_XT))
                wait_free(pe, at)
                for k in range(KD):
                    ins = pe.matmul(bank[half][:, :], xnT[:, par, k, 0, :], w_in[:, k, D * half:D * half + D],
                                    start=(k == 0), stop=(k == KD - 1))
                filled(ins, at)

            def encode(blk, par, n):
                at = (blk, FILL_ENC + n)
                if n == 0:
                    wait_drained(pe, proj_fill(blk, FILL_XT))
                    wait_drained(pe, proj_fill(blk, FILL_XT + 1))
                wait_free(pe, at)
                for half in range(2):
                    m = 2 * n + half
                    for k in range(KD):
                        ins = pe.matmul(bank[n % 2][:, T2 * half:T2 * half + T2], w_enc[:, k, P * m:P * m + P],
                                        xnT[:, par, k, :, :], start=(k == 0), stop=(k == KD - 1))
                filled(ins, at)

            def controller(blk):
                wait_drained(pe, (blk, FILL_ENC + 2))
                wait_drained(pe, (blk, FILL_ENC + 3))
                for q in range(2):
                    pe.matmul(cont_acc[:, q, :], ones[64:65, :], bias_rows[64:65, 0:MA], start=True, stop=False)
                    for k in range(KH):
                        ins = pe.matmul(cont_acc[:, q, :], wide[:, k, P * q:P * q + P], w_s2c[:, k, :],
                                        start=False, stop=(k == KH - 1))
                ins.then_inc(cont_ready, 1)

            def contT_transpose(blk):
                at = (blk, FILL_CONT)
                pe.wait_ge(cont_copied, blk + 1)
                wait_free(pe, at)
                for q in range(2):
                    ins = pe.transpose(bank[0][0:MA, P * q:P * q + P], cont[:, q, :], ident[:, :])
                filled(ins, at)

            def router(blk):
                wait_drained(pe, (blk, FILL_CONT))
                for q in range(2):
                    ins = pe.matmul(logit_acc[:, q, :], contT[:, P * q:P * q + P], w_r[:, :], start=True, stop=True)
                ins.then_inc(logits_ready, 1)

            def gateT_transpose(blk):
                at = (blk, FILL_GATE)
                pe.wait_ge(gate_ready, blk + 1)
                wait_free(pe, at)
                for q in range(2):
                    ins = pe.transpose(bank[1][0:E, P * q:P * q + P], gate[:, q, :], ident[:, :])
                filled(ins, at)

            def conteT_transpose(blk, n):
                at = (blk, FILL_CONTE + n)
                pe.wait_ge(conte_ready, blk + 1)
                wait_free(pe, at)
                for e in range(2):
                    for q in range(2):
                        c0 = T2 * e + P * q
                        ins = pe.transpose(bank[n % 2][0:MA, c0:c0 + P], conte[:, q, 2 * n + e, :], ident[:, :])
                filled(ins, at)

            def expert_up(blk, n):
                at = (blk, FILL_W1[n])
                e = n // 2
                if n % 4 == 0:
                    wait_drained(pe, (blk, FILL_CONTE + n // 4))
                wait_free(pe, at)
                for half in range(2):
                    t = 2 * (n % 2) + half
                    ins = pe.matmul(bank[n % 2][:, T2 * half:T2 * half + T2], w_1[:, e, P * t:P * t + P],
                                    conteT[:, e, :], start=True, stop=True)
                filled(ins, at)

            def expert_down(blk, n):
                if n == 0:
                    wait_drained(pe, (blk, FILL_GATE))
                    pe.matmul(eo_acc[0:M, :], bias_2[:, :], gateT[:, :], start=True, stop=False)
                wait_drained(pe, (blk, FILL_W1[n]))
                for half in range(2):
                    t = 2 * (n % 2) + half
                    ins = pe.matmul(eo_acc[M * half:M * half + M, :], w_2[:, 4 * (n // 2) + t, :],
                                    hT[:, n % 2, T2 * half:T2 * half + T2],
                                    start=(n == 0 and half == 1), stop=(n == 15))
                if n == 15:
                    ins.then_inc(eo_ready, 1)

            def experts(blk, a, b):
                for n in range(a, b):
                    expert_up(blk, n)
                    if n > 0:
                        expert_down(blk, n - 1)

            def to_spikes(blk, n):
                at = (blk, FILL_C2S + n)
                if n == 0:
                    pe.wait_ge(eo_copied, blk + 1)
                wait_free(pe, at)
                for half in range(2):
                    m = 2 * n + half
                    ins = pe.matmul(bank[n % 2][:, T2 * half:T2 * half + T2], w_c2s[:, P * m:P * m + P],
                                    eoT[:, :], start=True, stop=True)
                filled(ins, at)

            def decode(blk, q):
                at = (blk, FILL_DEC + q)
                if q == 0:
                    wait_drained(pe, (blk, FILL_C2S + 2))
                    wait_drained(pe, (blk, FILL_C2S + 3))
                wait_free(pe, at)
                pe.matmul(bank[q][:, :], ones[0:1, :], bias_rows[0:1, :], start=True, stop=False)
                for k in range(KH):
                    ins = pe.matmul(bank[q][:, :], wide[:, k, P * q:P * q + P], w_dec[:, k, :],
                                    start=False, stop=(k == KH - 1))
                filled(ins, at)

            def fin_transpose(blk):
                at = fin_fill(blk, FILL_FIN)
                pe.wait_ge(o_ready, blk + 1)
                wait_free(pe, at)
                for k in range(KD):
                    ins = pe.transpose(bank[0][:, P * k:P * k + P], o[:, P * k:P * k + P], ident[:, :])
                filled(ins, at)

            def fin_out(blk):
                at = fin_fill(blk, FILL_FIN + 1)
                wait_drained(pe, fin_fill(blk, FILL_FIN))
                wait_free(pe, at)
                pe.matmul(bank[1][:, :], ones[32:33, :], bias_rows[32:33, :], start=True, stop=False)
                for k in range(KD):
                    ins = pe.matmul(bank[1][:, :], oT[:, k, :], w_out[:, k, :], start=False, stop=(k == KD - 1))
                filled(ins, at)

            pe.wait_ge(weights_loaded, ALL_LOADED)
            pe.wait_ge(consts_made, 1)
            pe.wait_ge(pool_made, 8)
            cm = h[:, 1, 0, 0:KD * S].rearrange("p (k s) -> p k s", k=KD)
            for f in range(F):
                for b in range(B):
                    for k in range(KD):
                        ins = pe.matmul(ps_acc[SP * b:SP * b + SP, f:f + 1], cm[:, k, SP * f:SP * f + SP],
                                        ones[:, 0:1], start=(k == 0), stop=(k == KD - 1))
            ins.then_inc(c_summed, 1)
            proj_transpose(0, 0)
            proj_transpose(0, 1)
            pe.wait_ge(ready, 2)
            proj_in(0, 0, 0)
            proj_in(0, 0, 1)

            def body(blk, par):
                for tau in range(STEPS):
                    if tau == 1 and not is_first(blk):
                        y(blk - 1, NQ - 1)
                    if tau >= 5 and tau % QUAD == 1:
                        y(blk, (tau - 5) // QUAD)
                    if tau in (0, 1, 2):
                        encode(blk, par, tau)
                    if tau == 4:
                        encode(blk, par, 3)
                    if tau == 6:
                        controller(blk)
                    if tau == 7 and not is_first(blk):
                        fin_transpose(blk - 1)
                    if tau == 8:
                        if not is_first(blk):
                            fin_out(blk - 1)
                        contT_transpose(blk)
                    if tau == 9:
                        router(blk)
                    if tau == 13:
                        gateT_transpose(blk)
                    if tau == 14:
                        for n in range(4):
                            conteT_transpose(blk, n)
                    if tau == 15:
                        experts(blk, 0, 2)
                    if tau == 16:
                        experts(blk, 2, 4)
                    if tau == 18:
                        experts(blk, 4, 6)
                    if tau == 19:
                        experts(blk, 6, 8)
                        if not is_last(blk):
                            proj_transpose(blk + 1, 0)
                            proj_transpose(blk + 1, 1)
                    if tau == 20:
                        experts(blk, 8, 10)
                    if tau == 21:
                        experts(blk, 10, 12)
                    if tau == 22 and not is_last(blk):
                        proj_in(blk + 1, 1 - par, 0)
                        proj_in(blk + 1, 1 - par, 1)
                    if tau == 24:
                        experts(blk, 12, 14)
                    if tau == 25:
                        experts(blk, 14, 16)
                        expert_down(blk, 15)
                    if tau == 26:
                        to_spikes(blk, 0)
                        to_spikes(blk, 1)
                    if tau == 27:
                        to_spikes(blk, 2)
                        to_spikes(blk, 3)
                    if tau == 28:
                        decode(blk, 0)
                    if tau == 31:
                        decode(blk, 1)

            run_bodies(pe, body)
            y(LAST, NQ - 1)
            fin_transpose(LAST)
            fin_out(LAST)

        @block.vector
        def _(dve):
            def step(blk, tau):
                t2 = 2 * STEPS * blk + 2 * tau
                for f in range(F):
                    if not (is_first(blk) and tau == 0):
                        dve.wait_ge(h_ready, t2 - 1 + f)
                    dve.tensor_tensor(ps_z[:, f, :], h[:, (tau - 1) % RING, f, :], ps_A[:, f, :],
                                      ALU.mult).then_inc(m_done, 1)
                for f in range(F):
                    if f == 0:
                        dve.wait_ge(u_ready, STEPS * blk + tau + 1)
                    dve.wait_ge(m_done, t2 + f + 1)
                    dve.tensor_tensor(ps_z[:, f, :], ps_z[:, f, :], u[:, tau % 2, f, :],
                                      ALU.add).then_inc(z_ready, 1)

            def proj_stats(blk):
                dve.wait_ge(x_loaded, 16 * QUAD * (x_load_number(blk, False) + 1))
                for q in range(2):
                    dve.bn_stats(p_st[:, q, :], xbuf[:, q, :]).then_inc(p_stats_done, 1)
                dve.wait_ge(p_stats_done, 4 * blk + 2)
                dve.sem_inc(stats_settled, 1)
                for q in range(2):
                    dve.bn_aggr(p_mv[:, q, :], p_st[:, q, :]).then_inc(p_stats_done, 1)

            def proj_evac(blk, par, half):
                at = proj_fill(blk, FILL_WIN + half)
                wait_filled(dve, at)
                dve.wait_ge(p_scale_steps, 8 * blk + 8)
                dst = (xp, gt)[half]
                drained(dve.scalar_tensor_tensor(out=dst[:, par, :], in0=bank[half][:, :], scalar=p_rr[:, 0:1],
                                                 in1=b_in_all[:, D * half:D * half + D],
                                                 op0=ALU.mult, op1=ALU.add), at)

            def route(blk):
                def wait_link(n):
                    dve.wait_ge(route_steps, 9 * blk + n)

                dve.wait_ge(logits_copied, blk + 1)
                others = logit_acc.unsqueeze(2).to_broadcast([P, 2, E, E])
                own = logit[:, :, :].unsqueeze(3).to_broadcast([P, 2, E, E])
                for q in range(2):
                    dve.tensor_tensor(atleast[:, q], others[:, q], own[:, q], ALU.is_ge)
                    ins = dve.tensor_tensor(over[:, q], others[:, q], own[:, q], ALU.is_gt)
                ins.then_inc(route_steps, 1)
                wait_link(1)
                dve.tensor_tensor(atleast, atleast, before[:, :, :].unsqueeze(1).to_broadcast([P, 2, E, E]),
                                  ALU.mult).then_inc(route_steps, 1)
                wait_link(2)
                dve.tensor_tensor(atleast, atleast, over[:, :, :, :], ALU.max).then_inc(route_steps, 1)
                wait_link(3)
                dve.tensor_reduce(rank, atleast, AX.X, ALU.add).then_inc(route_steps, 1)
                wait_link(4)
                dve.tensor_scalar(sel[:, :, :], rank, 1.5, None, ALU.is_lt).then_inc(route_steps, 1)
                wait_link(5)
                dve.tensor_tensor(selected, logit_acc, sel[:, :, :], ALU.mult).then_inc(route_steps, 1)
                wait_link(6)
                dve.tensor_reduce(top_sum[:, :], selected, AX.X, ALU.add).then_inc(route_steps, 1)
                wait_link(7)
                dve.scalar_tensor_tensor(out=margin, in0=logit_acc, scalar=2.0,
                                         in1=top_sum[:, :].unsqueeze(2).to_broadcast([P, 2, E]),
                                         op0=ALU.mult, op1=ALU.subtract).then_inc(route_steps, 1)

            def route_gate(blk):
                dve.wait_ge(weight_ready, blk + 1)
                dve.tensor_tensor(gate[:, :, :], weight, sel[:, :, :], ALU.mult).then_inc(gate_ready, 1)
                dve.wait_ge(gate_ready, blk + 1)
                dve.sem_inc(route_steps, 1)

            def dec_stats(blk, q):
                t = 2 * blk + q
                wait_filled(dve, (blk, FILL_DEC + q))
                dve.bn_stats(d_st[:, q, :], bank[q][:, :]).then_inc(d_stats_done, 1)
                dve.wait_ge(d_stats_done, 2 * t + 1)
                dve.sem_inc(stats_settled, 1)
                dve.bn_aggr(d_mv[:, q, :], d_st[:, q, :]).then_inc(d_stats_done, 1)

            def fin_y(blk):
                dve.wait_ge(t1_ready, blk + 1)
                dve.wait_ge(y_done, NQ * (blk + 1))
                dve.tensor_tensor(o, ps_y[:, :], o, ALU.add).then_inc(y_taken, 1)

            def fin_mul(blk):
                at = fin_fill(blk, FILL_FIN + 1)
                wait_filled(dve, at)
                dve.wait_ge(sg_used, sg_number(blk, 1) + 1)
                dve.tensor_tensor(g[:, 0, :], bank[1][:, :], g[:, 0, :], ALU.mult).then_inc(g_times_s, 1)
                dve.tensor_tensor(g[:, 1, :], bank[1][:, :], g[:, 1, :], ALU.mult).then_inc(g_times_s, 1)
                dve.wait_ge(g_times_s, 2 * blk + 2)
                dve.sem_inc(bank_drained[1], 1)

            dve.memset(ones[:, :], 1.0)
            dve.memset(c_wide[:, :, :], 0.0)
            dve.memset(h[:, RING - 1, :, :], 0.0)
            dve.memset(bias_rows[64:65, M:MA], 1.0)
            dve.memset(w_s2c[:, :, M:MA], 0.0).then_inc(consts_made, 1)
            dve.wait_ge(consts_made, 1)
            proj_stats(0)
            dve.wait_ge(weights_loaded, ALL_LOADED)
            dve.wait_ge(c_summed, 1)
            for k in range(KD):
                dve.tensor_scalar(w_in[:, k, :], w_in[:, k, :], g_col[:, k:k + 1], None, ALU.mult)
            for b in range(B):
                rows = slice(SP * b, SP * b + SP)
                ins = dve.tensor_copy(c_wide[rows, :, SP - 4 + b:SP - 3 + b],
                                      ps_acc[rows, 0:F].unsqueeze(2))
            ins.then_inc(ready, 1)
            proj_evac(0, 0, 0)
            proj_evac(0, 0, 1)
            dve.wait_ge(ready, 2)

            def body(blk, par):
                for tau in range(STEPS):
                    step(blk, tau)
                    if not is_first(blk):
                        if tau == 1:
                            dec_stats(blk - 1, 1)
                        if tau == 3:
                            fin_y(blk - 1)
                        if tau == 11:
                            fin_mul(blk - 1)
                    if tau == 12:
                        route(blk)
                    if tau == 13:
                        route_gate(blk)
                    if not is_last(blk):
                        if tau == 16:
                            proj_stats(blk + 1)
                        if tau == 24:
                            proj_evac(blk + 1, 1 - par, 0)
                        if tau == 25:
                            proj_evac(blk + 1, 1 - par, 1)
                    if tau == 31:
                        dec_stats(blk, 0)

            run_bodies(dve, body)
            dec_stats(LAST, 1)
            fin_y(LAST)
            fin_mul(LAST)


_PRE = "L0_attn_"
_FFN = "L0_ffn_"
_ORDER = [_PRE + n for n in ("x", "w_in", "b_in", "A", "Bm", "Cm", "Dv", "w_out", "b_out", "g_norm")] + \
         [_FFN + n for n in ("W_enc", "b_enc", "W_s2c", "b_s2c", "Wr", "br", "W1", "b1", "W2", "b2",
                             "W_c2s", "b_c2s", "W_dec", "b_dec", "ln_g", "ln_b")]
_TRANSPOSED = {_PRE + "w_in", _PRE + "A", _PRE + "Bm", _PRE + "w_out"}
_COLUMNS = {_PRE + "g_norm", _FFN + "b_enc", _FFN + "b_c2s"}


def lay_out(name, a):
    if name in _TRANSPOSED:
        a = a.T
    if name in _COLUMNS:
        a = a.reshape(-1, P).T
    return np.ascontiguousarray(a)


def kernel(**inputs):
    import concourse.bacc as _bacc
    from concourse.bass_utils import run_bass_kernel_spmd as _run

    nc = _bacc.Bacc("TRN2", target_bir_lowering=False, num_devices=1)
    arrays, args = {}, []
    for name in _ORDER:
        a = lay_out(name, np.asarray(inputs[name]))
        arrays[f"in_{name}"] = a
        args.append(nc.dram_tensor(f"in_{name}", a.shape, mybir.dt.from_np(a.dtype), kind="ExternalInput").ap())
    out = nc.dram_tensor("out_0", inputs[_ORDER[0]].shape, F32, kind="ExternalOutput").ap()
    build(nc, *args, out)
    r = _run(nc, [arrays], core_ids=[0])
    return r.results[0]["out_0"]
```

```python
from contextlib import ExitStack

import numpy as np

import concourse.bass as bass
from concourse import mybir

F32 = mybir.dt.float32
ALU = mybir.AluOpType
ACT = mybir.ActivationFunctionType
AX = mybir.AxisListType

P = 128
B = 4
D = 512
S = 64
SP = 32
F = S // SP
STEPS = 32
QUAD = 4
NQ = STEPS // QUAD
CK = 4
RING = 8
KD = D // P
H = 1024
KH = H // P
M = 64
MA = M + 1
E = 8
EH = 512
T2 = 2 * P
NFILL = 34
LN_EPS = 1e-5
RMS_EPS = 1e-6

FILL_ENC, FILL_FIN, FILL_XT, FILL_WIN, FILL_CONTE, FILL_W1, FILL_C2S, FILL_DEC = 0, 4, 6, 8, 10, 14, 30, 33

SP_CHUNK = (-10, 0, 9, 10, 12, 12, 12, 12)
SP_X = -31
SP_STORE_SCRATCH = -17
SP_RESIDUAL = (36, 48)
SP_STORE_OUT = 55
POOL_PROJ_SCALE = -25
POOL_GATE_MUL = -3
POOL_DEC_SCALE = (32, 35)
POOL_DEC_SILU = (38, 40)
POOL_FIN_SKIP = 31
POOL_FIN_GATE = 36
POOL_FIN_ADD = (53, 59)
ACT_PROJ_NORM = -24.5
ACT_PROJ_EVAC = (-24.5, -23.5)
ACT_GATE_SIG = -4
ACT_SPIKES = (0.5, 2.5, 3.5, 4.5)
ACT_CONTT_COPY = 5.5
ACT_LOGITS_COPY = 6.5
ACT_ROUTE_SIG = 9.5
ACT_SCALE_CONT = (9.5, 10.5)
ACT_CONTET_COPY = (11.5, 11.5, 12.5, 12.5)
ACT_GATET_COPY = 12.5
ACT_RELU = (13.5, 13.5, 14.5, 14.5, 15.5, 15.5, 16.5, 16.5, 17.5, 17.5, 18.5, 19.5, 20, 20.5, 21.5, 21.5)
ACT_EO_COPY = 22.5
ACT_SPIKES_AGAIN = (23.5, 24.5, 25.5, 25.5)
ACT_DEC_SIG = (35.5, 39)
ACT_FIN_EVAC = 38
PE_Y = (5, 15, 18, 22, 29, 32, 34, 36)
PE_PROJ_TRANSPOSE = (-22, -21)
PE_PROJ_IN = (-20, -18)
PE_ENCODE = (2, 4, 4, 4)
PE_CONTROLLER = 6
PE_ROUTER = 8
PE_CONTET = (17, 17, 18, 18)
PE_GATET = 18
PE_EXPERTS = (19, 19, 19, 19, 19, 19, 19, 19, 19, 19, 19, 20, 22, 22, 24, 28, 28)
PE_TO_SPIKES = (31, 31, 31, 31)
PE_DECODE = (33, 33)
PE_FIN_TRANSPOSE = 39
PE_FIN_OUT = 41
DVE_PROJ_STATS = -25.5
DVE_PROJ_EVAC = (-21.25, -20.25)
DVE_ROUTE = (7.25, 7.5, 7.75, 7.75, 8, 8.25, 9, 9.75)
DVE_ROUTE_GATE = 10
DVE_DEC_STATS = (28.75, 31.75)
DVE_DEC_CENTRE = (30.75, 36.75)
DVE_DEC_NORM = (32.75, 37.75)
DVE_FIN_Y = 34.75
DVE_FIN_MUL = 40.5
DVE_PROJ_AGGR = -25.5
DVE_DEC_AGGR = (29.75, 33.75)


def build(nc, x, w_inT, b_in, A_T, B_T, Cm, Dv, w_outT, b_out, g_norm, W_enc, b_enc, W_s2c, b_s2c,
          Wr, br, W1, b1, W2, b2, W_c2s, b_c2s, W_dec, b_dec, ln_g, ln_b, out):
    NB = x.shape[1] // (2 * STEPS)
    LAST = NB - 1
    LT = NB * STEPS

    x_rows = x.rearrange("b (i m j q) d -> i j m b (q d)", m=NQ, j=QUAD, q=2)
    out_rows = out.rearrange("b (i m j q) d -> i j m b (q d)", m=NQ, j=QUAD, q=2)
    scratch = nc.dram_tensor("x_proj_scratch", (B, LT, D), F32, kind="Internal").ap()
    scratch_rows = scratch.rearrange("b (i m j) d -> i j m b d", m=NQ, j=QUAD)
    scratch_chunk = scratch.rearrange("b (i c t) d -> i c b (t d)", c=STEPS // CK, t=CK)

    with ExitStack() as ctx:
        def sb(name, shape):
            return ctx.enter_context(nc.sbuf_tensor(name, shape, F32))

        def pb(name, shape):
            return ctx.enter_context(nc.psum_tensor(name, shape, F32))

        def sem(name):
            return ctx.enter_context(nc.semaphore(name))

        w_in = sb("w_in", [P, KD, 2 * D])
        w_out = sb("w_out", [P, KD, D])
        w_enc = sb("w_enc", [P, KD, H])
        w_s2c = sb("w_s2c", [P, KH, M])
        w_r = sb("w_r", [P, E])
        w_1 = sb("w_1", [P, E, EH])
        w_2 = sb("w_2", [P, E * EH // P, M])
        w_c2s = sb("w_c2s", [P, H])
        w_dec = sb("w_dec", [P, KH, D])
        bt = sb("bt", [P, F, D])
        bias_rows = sb("bias_rows", [P, D])
        ones = sb("ones", [P, P])
        b_in_all = sb("b_in_all", [P, 2 * D])
        ln_g_all = sb("ln_g_all", [P, D])
        ln_b_all = sb("ln_b_all", [P, D])
        dv_all = sb("dv_all", [P, D])
        b_enc_col = sb("b_enc_col", [P, KH])
        b_c2s_col = sb("b_c2s_col", [P, KH])
        g_col = sb("g_col", [P, KD])
        cont_bias = sb("cont_bias", [P, 1])
        ident = sb("ident", [P, P])
        ident_2 = sb("ident_2", [P, M])
        before = sb("before", [P, E, E])
        c_wide = sb("c_wide", [P, F, 2 * SP - 4])
        minus_half = sb("minus_half", [P, 2])
        minus_one = sb("minus_one", [P, 2])
        ln_eps = sb("ln_eps", [P, 2])
        rms_eps = sb("rms_eps", [P, 2])
        h = sb("h", [P, RING, F, D])
        xb = sb("xb", [P, 2, CK, D])
        u = sb("u", [P, 2, F, D])
        xbuf = sb("xbuf", [P, 2, D])
        xres = sb("xres", [P, D])
        xnT = sb("xnT", [P, 2, KD, 2, P])
        xp = sb("xp", [P, 2, D])
        gt = sb("gt", [P, 2, D])
        wide = sb("wide", [P, KH, T2])
        conte = sb("conte", [P, 2, E, MA])
        hT = sb("hT", [P, 2, 2 * T2])
        g = sb("g", [P, 2, D])
        sg = sb("sg", [P, D])
        logit = sb("logit", [P, 2, E])
        sel = sb("sel", [P, 2, E])
        over = sb("over", [P, 2, E, E])
        top_sum = sb("top_sum", [P, 2])
        gate = sb("gate", [P, 2, E])
        p_st = sb("p_st", [P, 2, 6])
        p_mv = sb("p_mv", [P, 2, 2])
        p_r = sb("p_r", [P, 2])
        p_nm = sb("p_nm", [P, 2])
        p_rr = sb("p_rr", [P, 2])
        d_st = sb("d_st", [P, 2, 6])
        d_mv = sb("d_mv", [P, 2, 2])
        d_r = sb("d_r", [P, 2])
        eoT = hT[:, 0, 0:T2]
        contT = hT[:, 1, 0:T2]
        gateT = w_1[96:96 + E, 0, 0:T2]
        bias_2 = w_1[96:96 + E, 1, 0:M]
        conteT = wide[0:MA, :, :].rearrange("p (e) t -> p e t", e=E)
        conte_flat = conte[:, :, :, :].rearrange("p q e m -> p (q e m)")
        o = conte_flat[:, 0:D]
        oT = conte_flat[:, D:2 * D].rearrange("p (k t) -> p k t", k=KD)

        ps_A = pb("ps_A", [P, F, D])
        ps_z = pb("ps_z", [P, F, D])
        ps_y = pb("ps_y", [P, D])
        bank = [pb("bank0", [P, D]), pb("bank1", [P, D])]
        ps_acc = pb("ps_acc", [P, D])
        eo_acc = ps_acc[:, 0:T2]
        contT_acc = ps_acc[:, 0:T2]
        gateT_acc = ps_acc[0:E, 0:T2]
        cont_acc = ps_acc[:, T2:T2 + 2 * M].rearrange("p (q m) -> p q m", q=2)
        L0 = T2 + 2 * M
        logit_acc = ps_acc[:, L0:L0 + 2 * E].rearrange("p (q e) -> p q e", q=2)
        atleast = ps_acc[:, 0:2 * E * E].rearrange("p (q e j) -> p q e j", q=2, e=E)
        rank = ps_acc[:, 128:144].rearrange("p (q e) -> p q e", q=2)
        selected = ps_acc[:, 144:160].rearrange("p (q e) -> p q e", q=2)
        margin = ps_acc[:, 160:176].rearrange("p (q e) -> p q e", q=2)
        weight = ps_acc[:, 176:192].rearrange("p (q e) -> p q e", q=2)

        weights_loaded = sem("weights_loaded")
        consts_made = sem("consts_made")
        pool_made = sem("pool_made")
        c_summed = sem("c_summed")
        ready = sem("ready")
        bank_filled = [sem("bank0_filled"), sem("bank1_filled")]
        bank_drained = [sem("bank0_drained"), sem("bank1_drained")]
        acc_filled = sem("acc_filled")
        acc_drained = sem("acc_drained")
        u_ready = sem("u_ready")
        m_done = sem("m_done")
        z_ready = sem("z_ready")
        h_ready = sem("h_ready")
        y_done = sem("y_done")
        stats_settled = sem("stats_settled")
        y_taken = sem("y_taken")
        chunk_loaded = [sem("chunk0_loaded"), sem("chunk1_loaded")]
        x_loaded = sem("x_loaded")
        scratch_stored = sem("scratch_stored")
        out_stored = sem("out_stored")
        p_stats_done = sem("p_stats_done")
        p_scale_steps = sem("p_scale_steps")
        p_normed = sem("p_normed")
        gate_sigmoid = sem("gate_sigmoid")
        sg_used = sem("sg_used")
        contT_ready = sem("contT_ready")
        contT_copied = sem("contT_copied")
        gateT_ready = sem("gateT_ready")
        gateT_copied = sem("gateT_copied")
        logits_ready = sem("logits_ready")
        logits_copied = sem("logits_copied")
        route_steps = sem("route_steps")
        weight_ready = sem("weight_ready")
        gate_ready = sem("gate_ready")
        conte_ready = sem("conte_ready")
        eo_ready = sem("eo_ready")
        eo_copied = sem("eo_copied")
        d_stats_done = sem("d_stats_done")
        d_scale_steps = sem("d_scale_steps")
        d_centred = sem("d_centred")
        g_sigmoid = sem("g_sigmoid")
        t1_ready = sem("t1_ready")
        o_ready = sem("o_ready")
        g_times_s = sem("g_times_s")
        tile_ready = sem("tile_ready")
        residual_loaded = sem("residual_loaded")

        n_loads = [0]

        def fill_number(blk, k):
            if isinstance(blk, int) and blk == 0:
                return 4 + k - (2 if k >= FILL_XT else 0)
            if isinstance(blk, int) and blk == LAST:
                return NFILL * blk + 2 + k - (4 if k >= FILL_CONTE else 0)
            return NFILL * blk + 2 + k

        def fill_count(n_or_blk, k):
            if isinstance(n_or_blk, int):
                return fill_number(n_or_blk, k) // 2 + 1
            return (NFILL // 2) * n_or_blk + (2 + k) // 2 + 1

        def proj_fill(blk, k):
            if isinstance(blk, int) and blk == 0:
                return None, (k - FILL_XT if k < FILL_WIN else 2 + k - FILL_WIN)
            return blk - 1, k

        def fin_fill(blk, k):
            if isinstance(blk, int) and blk == LAST:
                return None, NFILL * (LAST + 1) - 2 + k - FILL_FIN
            return blk + 1, k

        def count_of(at):
            body, k = at
            return k // 2 + 1 if body is None else fill_count(body, k)

        def wait_filled(eng, at):
            eng.wait_ge(bank_filled[at[1] % 2], count_of(at))

        def wait_drained(eng, at):
            eng.wait_ge(bank_drained[at[1] % 2], count_of(at))

        def wait_free(eng, at):
            if at[0] is None and at[1] < 2:
                return
            eng.wait_ge(bank_drained[at[1] % 2], count_of(at) - 1)

        def filled(ins, at):
            ins.then_inc(bank_filled[at[1] % 2], 1)

        def drained(ins, at):
            ins.then_inc(bank_drained[at[1] % 2], 1)

        dec_out = [bank[1], ps_acc]

        def wait_dec_filled(eng, blk, q):
            if q == 0:
                wait_filled(eng, (blk, FILL_DEC))
            else:
                eng.wait_ge(acc_filled, 2 * blk + 2)

        def wait_dec_drained(eng, blk, q):
            if q == 0:
                wait_drained(eng, (blk, FILL_DEC))
            else:
                eng.wait_ge(acc_drained, 2 * blk + 2)

        C2S_FILL = [FILL_C2S, FILL_C2S + 1, None, FILL_C2S + 2]

        def sg_number(blk, tile):
            if tile is None:
                return 0 if isinstance(blk, int) and blk == 0 else 3 * blk - 2
            if isinstance(blk, int) and blk == LAST:
                return 3 * blk + 1 + tile
            return 3 * blk + 2 + tile

        block = ctx.enter_context(nc.Block())

        def run_bodies(eng, steps, between, parts=1):
            def body(blk, par):
                for n in range(STEPS * parts):
                    slot = n / parts
                    steps(blk, slot)
                    if not is_first(blk):
                        between(blk - 1, 1 - par, slot + STEPS)
                    between(blk, par, slot)
                    if not is_last(blk):
                        between(blk + 1, 1 - par, slot - STEPS)

            body(0, 0)
            with eng.Fori(0, (LAST - 1) // 2) as pair:
                body(2 * pair + 1, 1)
                body(2 * pair + 2, 0)
            body(LAST, LAST % 2)
            for n in range(STEPS * parts):
                between(LAST, LAST % 2, STEPS + n / parts)

        def is_first(blk):
            return isinstance(blk, int) and blk == 0

        def is_last(blk):
            return isinstance(blk, int) and blk == LAST

        @block.sync
        def _(sp):
            def load(dst, src):
                sp.dma_start(dst, src).then_inc(weights_loaded, 16)
                n_loads[0] += 1

            def load_x(blk):
                if not is_first(blk):
                    for q in range(2):
                        wait_drained(sp, proj_fill(0 if isinstance(blk, int) and blk == 1 else blk - 1, FILL_XT + q))
                for j in range(QUAD):
                    sp.dma_start(xbuf[32 * j:32 * j + 32, :, :].rearrange("p q d -> p (q d)"),
                                 x_rows[blk, j]).then_inc(x_loaded, 16)

            def load_residual(blk, q):
                if not (is_first(blk) and q == 0):
                    sp.wait_ge(tile_ready, 1 + 2 * blk + q)
                for j in range(QUAD):
                    sp.dma_start(xres[32 * j:32 * j + 32, :],
                                 x_rows[blk, j][:, :, D * q:D * q + D]).then_inc(residual_loaded, 16)

            def store_scratch(blk, par):
                wait_drained(sp, proj_fill(blk, FILL_WIN))
                for j in range(QUAD):
                    sp.dma_start(scratch_rows[blk, j], xp[32 * j:32 * j + 32, par, :]
                                 ).then_inc(scratch_stored, 16)

            def load_chunk(blk, c):
                if not (is_first(blk) and c < 2):
                    sp.wait_ge(u_ready, STEPS * blk + CK * (c - 1))
                if c == 0:
                    sp.wait_ge(scratch_stored, 16 * QUAD * (blk + 1))
                for b in range(B):
                    sp.dma_start(xb[SP * b:SP * b + SP, c % 2, :, :].rearrange("p t d -> p (t d)"),
                                 scratch_chunk[blk, c, b].partition_broadcast(SP)
                                 ).then_inc(chunk_loaded[c % 2], 16)

            def store_out(blk):
                sp.wait_ge(tile_ready, 1 + 2 * blk + 2)
                for j in range(QUAD):
                    sp.dma_start(out_rows[blk, j],
                                 g[32 * j:32 * j + 32, :, :].rearrange("p q d -> p (q d)")
                                 ).then_inc(out_stored, 16)

            load_x(0)
            load(g_col[:, :], g_norm)
            load(w_in[:, :, :], w_inT.rearrange("(k p) n -> p k n", p=P))
            load(b_in_all[:, :], b_in.partition_broadcast(P))
            for b in range(B):
                load(h[SP * b:SP * b + SP, 0, :, :], A_T.rearrange("(f s) d -> s f d", f=F))
                load(bt[SP * b:SP * b + SP, :, :], B_T.rearrange("(f s) d -> s f d", f=F))
            load(h[:, 1, 0, 0:KD * S].rearrange("p (k s) -> p k s", k=KD), Cm.rearrange("(k p) s -> p k s", p=P))
            load(w_enc[:, :, :], W_enc.rearrange("(k p) n -> p k n", p=P))
            load(b_enc_col[:, :], b_enc)
            load(w_s2c[:, :, :], W_s2c.rearrange("(k p) n -> p k n", p=P))
            load(bias_rows[0:1, :], b_dec.partition_broadcast(1))
            load(bias_rows[32:33, :], b_out.partition_broadcast(1))
            load(bias_rows[64:65, 0:E], br.partition_broadcast(1))
            load(cont_bias[0:M, :], b_s2c)
            for half in range(2):
                load(w_r[M * half:M * half + M, :], Wr)
            load(w_1[0:M, :, :], W1.rearrange("e m h -> m e h"))
            load(w_1[M:MA, :, :].rearrange("p e h -> p (e h)"), b1.rearrange("e h -> (e h)").partition_broadcast(1))
            load(w_2[:, :, :], W2.rearrange("e (t p) m -> p (e t) m", p=P))
            load(bias_2, b2)
            for half in range(2):
                load(w_c2s[M * half:M * half + M, :], W_c2s)
            load(b_c2s_col[:, :], b_c2s)
            load(w_dec[:, :, :], W_dec.rearrange("(k p) n -> p k n", p=P))
            load(w_out[:, :, :], w_outT.rearrange("(k p) n -> p k n", p=P))
            load(ln_g_all[:, :], ln_g.partition_broadcast(P))
            load(ln_b_all[:, :], ln_b.partition_broadcast(P))
            load(dv_all[:, :], Dv.partition_broadcast(P))

            store_scratch(0, 0)
            load_chunk(0, 0)

            def between(blk, par, slot):
                for c in range(STEPS // CK):
                    if slot == SP_CHUNK[c]:
                        load_chunk(blk, c)
                if slot == SP_X:
                    load_x(blk)
                if slot == SP_STORE_SCRATCH:
                    store_scratch(blk, par)
                for q in range(2):
                    if slot == SP_RESIDUAL[q]:
                        load_residual(blk, q)
                if slot == SP_STORE_OUT:
                    store_out(blk)

            run_bodies(sp, lambda blk, slot: None, between)
            sp.wait_ge(out_stored, 1 + 16 * QUAD * NB)
            sp.wait_ge(scratch_stored, 16 * QUAD * NB)

        ALL_LOADED = 16 * n_loads[0]

        @block.gpsimd
        def _(pool):
            pool.memset(ident[:, :], 0.0).then_inc(pool_made, 1)
            pool.memset(before[:, :, :], 1.0).then_inc(pool_made, 1)
            pool.memset(minus_half[:, :], -0.5).then_inc(pool_made, 1)
            pool.memset(minus_one[:, :], -1.0).then_inc(pool_made, 1)
            pool.memset(ln_eps[:, :], LN_EPS).then_inc(pool_made, 1)
            pool.memset(rms_eps[:, :], RMS_EPS).then_inc(pool_made, 1)
            pool.wait_ge(pool_made, 6)
            pool.affine_select(out=ident[:, :], in_=ident[:, :], compare_op=ALU.not_equal, fill=1.0,
                               base=0, pattern=[[-1, P]], channel_multiplier=1).then_inc(pool_made, 1)
            pool.affine_select(out=before[:, :, :], in_=before[:, :, :], compare_op=ALU.is_ge, fill=0.0,
                               base=-1, pattern=[[1, E], [-1, E]], channel_multiplier=0).then_inc(pool_made, 1)

            def step(blk, slot):
                tau = int(slot)
                c = tau // CK
                if tau % CK == 0:
                    pool.wait_ge(chunk_loaded[c % 2], 16 * B * (4 * blk + c // 2 + 1))
                if not (is_first(blk) and tau < 2):
                    pool.wait_ge(z_ready, 2 * STEPS * blk + 2 * tau - 2)
                xt = xb[:, c % 2, tau % CK, :].unsqueeze(1).to_broadcast([P, F, D])
                pool.tensor_tensor(u[:, tau % 2, :, :], xt, bt[:, :, :], ALU.mult).then_inc(u_ready, 1)

            def proj_scale(blk):
                n = [0]

                def link(ins):
                    ins.then_inc(p_scale_steps, 1)
                    n[0] += 1

                def wait_link():
                    pool.wait_ge(p_scale_steps, 8 * blk + n[0])

                pool.wait_ge(p_stats_done, 4 * blk + 4)
                link(pool.tensor_tensor(p_rr[:, :], p_mv[:, :, 1], ln_eps[:, :], ALU.add))
                wait_link()
                link(pool.tensor_tensor(p_r[:, :], p_rr[:, :], minus_half[:, :], ALU.pow))
                wait_link()
                link(pool.tensor_tensor(p_nm[:, :], p_mv[:, :, 0], p_r[:, :], ALU.mult))
                wait_link()
                link(pool.tensor_tensor(p_nm[:, :], p_nm[:, :], minus_one[:, :], ALU.mult))
                link(pool.tensor_tensor(p_rr[:, :], p_mv[:, :, 1], p_r[:, :], ALU.mult))
                wait_link()
                link(pool.tensor_tensor(p_rr[:, :], p_rr[:, :], p_r[:, :], ALU.mult))
                wait_link()
                link(pool.tensor_tensor(p_rr[:, :], p_rr[:, :], rms_eps[:, :], ALU.add))
                wait_link()
                link(pool.tensor_tensor(p_rr[:, :], p_rr[:, :], minus_half[:, :], ALU.pow))

            def gate_mul(blk, par):
                pool.wait_ge(gate_sigmoid, blk + 1)
                pool.tensor_tensor(gt[:, par, :], gt[:, par, :], sg[:, :], ALU.mult).then_inc(sg_used, 1)

            def dec_scale(blk, q):
                t = 2 * blk + q
                pool.wait_ge(d_stats_done, 2 * t + 2)
                r = d_r[:, q:q + 1]
                pool.tensor_tensor(r, d_mv[:, q, 1:2], ln_eps[:, 0:1], ALU.add).then_inc(d_scale_steps, 1)
                pool.wait_ge(d_scale_steps, 2 * t + 1)
                pool.tensor_tensor(r, r, minus_half[:, 0:1], ALU.pow).then_inc(d_scale_steps, 1)

            def dec_silu(blk, q):
                pool.wait_ge(g_sigmoid, 2 * blk + q + 1)
                pool.tensor_tensor(g[:, q, :], g[:, q, :], sg[:, :], ALU.mult).then_inc(sg_used, 1)

            def fin_skip(blk, par):
                wait_filled(pool, (blk, FILL_CONTE + 3))
                pool.tensor_tensor(o, xp[:, par, :], dv_all[:, :], ALU.mult).then_inc(t1_ready, 1)

            def fin_gate(blk, par):
                pool.wait_ge(y_taken, blk + 1)
                pool.tensor_tensor(o, o, gt[:, par, :], ALU.mult).then_inc(o_ready, 1)

            def fin_add(blk, q):
                if q == 0:
                    pool.wait_ge(g_times_s, blk + 1)
                else:
                    wait_drained(pool, fin_fill(blk, FILL_FIN + 1))
                pool.wait_ge(residual_loaded, 16 * QUAD * (2 * blk + q + 1))
                pool.tensor_tensor(g[:, q, :], g[:, q, :], xres[:, :], ALU.add).then_inc(tile_ready, 1)

            pool.wait_ge(ready, 2)
            proj_scale(0)
            gate_mul(0, 0)

            def between(blk, par, slot):
                if slot == POOL_PROJ_SCALE:
                    proj_scale(blk)
                if slot == POOL_GATE_MUL:
                    gate_mul(blk, par)
                for q in range(2):
                    if slot == POOL_DEC_SCALE[q]:
                        dec_scale(blk, q)
                    if slot == POOL_DEC_SILU[q]:
                        dec_silu(blk, q)
                if slot == POOL_FIN_SKIP:
                    fin_skip(blk, par)
                if slot == POOL_FIN_GATE:
                    fin_gate(blk, par)
                for q in range(2):
                    if slot == POOL_FIN_ADD[q]:
                        fin_add(blk, q)

            run_bodies(pool, step, between)

        @block.scalar
        def _(act):
            def tanh(blk, slot):
                tau = int(slot)
                f = int(F * (slot - tau))
                act.wait_ge(z_ready, 2 * STEPS * blk + 2 * tau + f + 1)
                if f == 0 and tau % QUAD == 0 and not (is_first(blk) and tau < RING):
                    act.wait_ge(y_done, NQ * blk + tau // QUAD - 1)
                act.activation(h[:, tau % RING, f, :], ps_z[:, f, :], ACT.Tanh).then_inc(h_ready, 1)

            def proj_norm(blk):
                act.wait_ge(p_scale_steps, 8 * blk + 8)
                for q in range(2):
                    act.activation(xbuf[:, q, :], xbuf[:, q, :], ACT.Identity, bias=p_nm[:, q:q + 1],
                                   scale=p_r[:, q:q + 1]).then_inc(p_normed, 1)

            def proj_evac(blk, par, q):
                at = proj_fill(blk, FILL_XT + q)
                wait_filled(act, at)
                drained(act.activation(xnT[:, par, :, q, :],
                                       bank[q][:, :].rearrange("p (k t) -> p k t", k=KD), ACT.Copy), at)

            def gate_sig(blk, par):
                wait_drained(act, proj_fill(blk, FILL_WIN + 1))
                if not is_first(blk):
                    act.wait_ge(sg_used, sg_number(blk, None))
                act.activation(sg[:, :], gt[:, par, :], ACT.Sigmoid).then_inc(gate_sigmoid, 1)

            def sigmoids(src, k, bias):
                for half in range(2):
                    m = 2 * k + half
                    ins = act.activation(wide[:, m, :], src[:, T2 * half:T2 * half + T2],
                                         ACT.Sigmoid, bias=bias[:, m:m + 1])
                return ins

            def spikes(blk, k):
                at = (blk, FILL_ENC + k)
                wait_filled(act, at)
                drained(sigmoids(bank[k % 2], k, b_enc_col), at)

            def spikes_again(blk, k):
                if C2S_FILL[k] is None:
                    act.wait_ge(acc_filled, 2 * blk + 1)
                    sigmoids(ps_acc, k, b_c2s_col).then_inc(acc_drained, 1)
                else:
                    at = (blk, C2S_FILL[k])
                    wait_filled(act, at)
                    drained(sigmoids(bank[at[1] % 2], k, b_c2s_col), at)

            def contT_copy(blk):
                act.wait_ge(contT_ready, blk + 1)
                act.activation(contT, contT_acc, ACT.Identity, bias=cont_bias[:, :]).then_inc(contT_copied, 1)

            def logits_copy(blk):
                act.wait_ge(logits_ready, blk + 1)
                act.activation(logit[:, :, :], logit_acc, ACT.Copy).then_inc(logits_copied, 1)

            def route_sig(blk):
                act.wait_ge(route_steps, 8 * blk + 8)
                act.activation(weight, margin, ACT.Sigmoid).then_inc(weight_ready, 1)

            def scale_cont(blk, q):
                if q == 0:
                    act.wait_ge(gate_ready, blk + 1)
                    if not is_first(blk):
                        wait_filled(act, fin_fill(blk - 1, FILL_FIN + 1))
                act.activation(conte[:, q, :, M], gate[:, q, :], ACT.Copy)
                for e in range(E):
                    ins = act.activation(conte[:, q, e, 0:M], cont_acc[:, q, :], ACT.Copy,
                                         scale=gate[:, q, e:e + 1])
                ins.then_inc(conte_ready, 1)

            def gateT_copy(blk):
                act.wait_ge(gateT_ready, blk + 1)
                act.activation(gateT, gateT_acc, ACT.Copy).then_inc(gateT_copied, 1)

            def conteT_copy(blk, k):
                at = (blk, FILL_CONTE + k)
                wait_filled(act, at)
                drained(act.activation(conteT[:, 2 * k:2 * k + 2, :],
                                       bank[k % 2][0:MA, :].rearrange("p (e t) -> p e t", e=2), ACT.Copy), at)

            def relu(blk, n):
                at = (blk, FILL_W1 + n)
                wait_filled(act, at)
                drained(act.activation(hT[:, n % 2, :], bank[n % 2][:, :], ACT.Relu), at)

            def eo_copy(blk):
                act.wait_ge(eo_ready, blk + 1)
                act.activation(eoT, eo_acc, ACT.Copy).then_inc(eo_copied, 1)

            def dec_sig(blk, q):
                wait_dec_drained(act, blk, q)
                act.wait_ge(sg_used, sg_number(blk, q))
                act.activation(sg[:, :], g[:, q, :], ACT.Sigmoid).then_inc(g_sigmoid, 1)

            def fin_evac(blk):
                at = fin_fill(blk, FILL_FIN)
                wait_filled(act, at)
                drained(act.activation(oT, bank[0][:, :].rearrange("p (k t) -> p k t", k=KD), ACT.Copy), at)

            act.wait_ge(weights_loaded, ALL_LOADED)
            act.wait_ge(pool_made, 8)
            for half in range(2):
                rows = slice(M * half, M * half + M)
                act.activation(ident_2[rows, :], ident[rows, rows], ACT.Copy)
            act.activation(ps_A[:, 0, :], h[:, 0, 0, :], ACT.Copy)
            act.activation(ps_A[:, 1, :], h[:, 0, 1, :], ACT.Copy).then_inc(ready, 1)
            proj_norm(0)
            proj_evac(0, 0, 0)
            proj_evac(0, 0, 1)
            gate_sig(0, 0)

            def between(blk, par, slot):
                if slot == ACT_PROJ_NORM:
                    proj_norm(blk)
                for q in range(2):
                    if slot == ACT_PROJ_EVAC[q]:
                        proj_evac(blk, par, q)
                if slot == ACT_GATE_SIG:
                    gate_sig(blk, par)
                for k in range(4):
                    if slot == ACT_SPIKES[k]:
                        spikes(blk, k)
                if slot == ACT_CONTT_COPY:
                    contT_copy(blk)
                if slot == ACT_LOGITS_COPY:
                    logits_copy(blk)
                if slot == ACT_ROUTE_SIG:
                    route_sig(blk)
                for q in range(2):
                    if slot == ACT_SCALE_CONT[q]:
                        scale_cont(blk, q)
                for k in range(4):
                    if slot == ACT_CONTET_COPY[k]:
                        conteT_copy(blk, k)
                if slot == ACT_GATET_COPY:
                    gateT_copy(blk)
                for n in range(16):
                    if slot == ACT_RELU[n]:
                        relu(blk, n)
                if slot == ACT_EO_COPY:
                    eo_copy(blk)
                for k in range(4):
                    if slot == ACT_SPIKES_AGAIN[k]:
                        spikes_again(blk, k)
                for q in range(2):
                    if slot == ACT_DEC_SIG[q]:
                        dec_sig(blk, q)
                if slot == ACT_FIN_EVAC:
                    fin_evac(blk)

            run_bodies(act, tanh, between, parts=F)

        @block.tensor
        def _(pe):
            def y(blk, k):
                pe.wait_ge(h_ready, 2 * STEPS * blk + 2 * QUAD * (k + 1))
                if k == 0 and not is_first(blk):
                    pe.wait_ge(y_taken, blk)
                for f in range(F):
                    for j in range(QUAD):
                        ins = pe.matmul(ps_y[32 * j:32 * j + 32, :],
                                        c_wide[:, f, SP - 4 - 4 * k:2 * SP - 4 - 4 * k],
                                        h[:, (QUAD * k + j) % RING, f, :],
                                        start=(k == 0 and f == 0), stop=(k == NQ - 1 and f == F - 1))
                ins.then_inc(y_done, 1)

            def proj_transpose(blk, q):
                at = proj_fill(blk, FILL_XT + q)
                pe.wait_ge(p_normed, 2 * blk + q + 1)
                wait_free(pe, at)
                for k in range(KD):
                    ins = pe.transpose(bank[q][:, P * k:P * k + P], xbuf[:, q, P * k:P * k + P], ident[:, :])
                filled(ins, at)

            def proj_in(blk, par, half):
                at = proj_fill(blk, FILL_WIN + half)
                wait_drained(pe, proj_fill(blk, FILL_XT))
                wait_free(pe, at)
                for k in range(KD):
                    ins = pe.matmul(bank[half][:, :], xnT[:, par, k, 0, :], w_in[:, k, D * half:D * half + D],
                                    start=(k == 0), stop=(k == KD - 1))
                filled(ins, at)

            def encode(blk, par, n):
                at = (blk, FILL_ENC + n)
                if n == 0:
                    wait_drained(pe, proj_fill(blk, FILL_XT))
                    wait_drained(pe, proj_fill(blk, FILL_XT + 1))
                wait_free(pe, at)
                for half in range(2):
                    m = 2 * n + half
                    for k in range(KD):
                        ins = pe.matmul(bank[n % 2][:, T2 * half:T2 * half + T2], w_enc[:, k, P * m:P * m + P],
                                        xnT[:, par, k, :, :], start=(k == 0), stop=(k == KD - 1))
                filled(ins, at)

            def controller(blk):
                wait_drained(pe, (blk, FILL_ENC + 2))
                wait_drained(pe, (blk, FILL_ENC + 3))
                if not is_first(blk):
                    wait_dec_drained(pe, blk - 1, 1)
                for k in range(KH):
                    half = k % 2
                    ins = pe.matmul(contT_acc[M * half:M * half + M, :], w_s2c[:, k, :], wide[:, k, :],
                                    start=(k < 2), stop=(k >= KH - 2))
                ins.then_inc(contT_ready, 1)

            def router(blk):
                pe.wait_ge(contT_copied, blk + 1)
                for q in range(2):
                    tokens = contT[:, P * q:P * q + P]
                    pe.matmul(logit_acc[:, q, :], ones[64:65, :], bias_rows[64:65, 0:E], start=True, stop=False)
                    pe.matmul(logit_acc[:, q, :], tokens, w_r[:, :], start=False, stop=True)
                    ins = pe.matmul(cont_acc[:, q, :], tokens, ident_2[:, :], start=True, stop=True)
                ins.then_inc(logits_ready, 1)

            def gateT_transpose(blk):
                pe.wait_ge(conte_ready, 2 * blk + 2)
                for q in range(2):
                    ins = pe.transpose(gateT_acc[:, P * q:P * q + P], gate[:, q, :], ident[:, :])
                ins.then_inc(gateT_ready, 1)

            def conteT_transpose(blk, n):
                at = (blk, FILL_CONTE + n)
                pe.wait_ge(conte_ready, 2 * blk + 2)
                wait_free(pe, at)
                for e in range(2):
                    for q in range(2):
                        c0 = T2 * e + P * q
                        ins = pe.transpose(bank[n % 2][0:MA, c0:c0 + P], conte[:, q, 2 * n + e, :], ident[:, :])
                filled(ins, at)

            def expert_up(blk, n):
                at = (blk, FILL_W1 + n)
                e = n // 2
                if n % 4 == 0:
                    wait_drained(pe, (blk, FILL_CONTE + n // 4))
                wait_free(pe, at)
                for half in range(2):
                    t = 2 * (n % 2) + half
                    ins = pe.matmul(bank[n % 2][:, T2 * half:T2 * half + T2], w_1[0:MA, e, P * t:P * t + P],
                                    conteT[:, e, :], start=True, stop=True)
                filled(ins, at)

            def expert_down(blk, n):
                if n == 0:
                    pe.wait_ge(gateT_copied, blk + 1)
                    pe.matmul(eo_acc[0:M, :], bias_2, gateT, start=True, stop=False)
                wait_drained(pe, (blk, FILL_W1 + n))
                for half in range(2):
                    t = 2 * (n % 2) + half
                    ins = pe.matmul(eo_acc[M * half:M * half + M, :], w_2[:, 4 * (n // 2) + t, :],
                                    hT[:, n % 2, T2 * half:T2 * half + T2],
                                    start=(n == 0 and half == 1), stop=(n == 15))
                if n == 15:
                    ins.then_inc(eo_ready, 1)

            def experts(blk, n):
                if n < 16:
                    expert_up(blk, n)
                if n > 0:
                    expert_down(blk, n - 1)

            def to_spikes(blk, n):
                if n == 0:
                    pe.wait_ge(eo_copied, blk + 1)
                at = None if C2S_FILL[n] is None else (blk, C2S_FILL[n])
                if at:
                    wait_free(pe, at)
                dst = bank[at[1] % 2] if at else ps_acc
                for half in range(2):
                    m = 2 * n + half
                    ins = pe.matmul(dst[:, T2 * half:T2 * half + T2], w_c2s[:, P * m:P * m + P],
                                    eoT, start=True, stop=True)
                if at:
                    filled(ins, at)
                else:
                    ins.then_inc(acc_filled, 1)

            def decode(blk, q):
                if q == 0:
                    wait_free(pe, (blk, FILL_DEC))
                else:
                    pe.wait_ge(acc_drained, 2 * blk + 1)
                dst = dec_out[q]
                pe.matmul(dst[:, :], ones[0:1, :], bias_rows[0:1, :], start=True, stop=False)
                for k in range(KH):
                    if q == 0 and k % 2 == 0:
                        if C2S_FILL[k // 2] is None:
                            pe.wait_ge(acc_drained, 2 * blk + 1)
                        else:
                            wait_drained(pe, (blk, C2S_FILL[k // 2]))
                    ins = pe.matmul(dst[:, :], wide[:, k, P * q:P * q + P], w_dec[:, k, :],
                                    start=False, stop=(k == KH - 1))
                if q == 0:
                    filled(ins, (blk, FILL_DEC))
                else:
                    ins.then_inc(acc_filled, 1)

            def fin_transpose(blk):
                at = fin_fill(blk, FILL_FIN)
                pe.wait_ge(o_ready, blk + 1)
                wait_free(pe, at)
                for k in range(KD):
                    ins = pe.transpose(bank[0][:, P * k:P * k + P], o[:, P * k:P * k + P], ident[:, :])
                filled(ins, at)

            def fin_out(blk):
                at = fin_fill(blk, FILL_FIN + 1)
                wait_drained(pe, fin_fill(blk, FILL_FIN))
                wait_free(pe, at)
                pe.matmul(bank[1][:, :], ones[32:33, :], bias_rows[32:33, :], start=True, stop=False)
                for k in range(KD):
                    ins = pe.matmul(bank[1][:, :], oT[:, k, :], w_out[:, k, :], start=False, stop=(k == KD - 1))
                filled(ins, at)

            pe.wait_ge(weights_loaded, ALL_LOADED)
            pe.wait_ge(consts_made, 1)
            pe.wait_ge(pool_made, 8)
            cm = h[:, 1, 0, 0:KD * S].rearrange("p (k s) -> p k s", k=KD)
            for f in range(F):
                for b in range(B):
                    for k in range(KD):
                        ins = pe.matmul(ps_acc[SP * b:SP * b + SP, f:f + 1], cm[:, k, SP * f:SP * f + SP],
                                        ones[:, 0:1], start=(k == 0), stop=(k == KD - 1))
            ins.then_inc(c_summed, 1)
            proj_transpose(0, 0)
            proj_transpose(0, 1)
            pe.wait_ge(ready, 2)
            proj_in(0, 0, 0)
            proj_in(0, 0, 1)

            def between(blk, par, slot):
                for k in range(NQ):
                    if slot == PE_Y[k]:
                        y(blk, k)
                for q in range(2):
                    if slot == PE_PROJ_TRANSPOSE[q]:
                        proj_transpose(blk, q)
                for half in range(2):
                    if slot == PE_PROJ_IN[half]:
                        proj_in(blk, par, half)
                for n in range(4):
                    if slot == PE_ENCODE[n]:
                        encode(blk, par, n)
                if slot == PE_CONTROLLER:
                    controller(blk)
                if slot == PE_ROUTER:
                    router(blk)
                for n in range(4):
                    if slot == PE_CONTET[n]:
                        conteT_transpose(blk, n)
                if slot == PE_GATET:
                    gateT_transpose(blk)
                for n in range(17):
                    if slot == PE_EXPERTS[n]:
                        experts(blk, n)
                for n in range(4):
                    if slot == PE_TO_SPIKES[n]:
                        to_spikes(blk, n)
                for q in range(2):
                    if slot == PE_DECODE[q]:
                        decode(blk, q)
                if slot == PE_FIN_TRANSPOSE:
                    fin_transpose(blk)
                if slot == PE_FIN_OUT:
                    fin_out(blk)

            run_bodies(pe, lambda blk, slot: None, between)

        @block.vector
        def _(dve):
            def step(blk, slot):
                tau = int(slot)
                t2 = 2 * STEPS * blk + 2 * tau
                part = int(2 * F * (slot - tau))
                f = part % F
                if part < F:
                    if not (is_first(blk) and tau == 0):
                        dve.wait_ge(h_ready, t2 - 1 + f)
                    dve.tensor_tensor(ps_z[:, f, :], h[:, (tau - 1) % RING, f, :], ps_A[:, f, :],
                                      ALU.mult).then_inc(m_done, 1)
                else:
                    if f == 0:
                        dve.wait_ge(u_ready, STEPS * blk + tau + 1)
                    dve.wait_ge(m_done, t2 + f + 1)
                    dve.tensor_tensor(ps_z[:, f, :], ps_z[:, f, :], u[:, tau % 2, f, :],
                                      ALU.add).then_inc(z_ready, 1)

            def proj_stats(blk):
                dve.wait_ge(x_loaded, 16 * QUAD * (blk + 1))
                for q in range(2):
                    dve.bn_stats(p_st[:, q, :], xbuf[:, q, :]).then_inc(p_stats_done, 1)

            def proj_aggr(blk):
                dve.wait_ge(p_stats_done, 4 * blk + 2)
                dve.sem_inc(stats_settled, 1)
                for q in range(2):
                    dve.bn_aggr(p_mv[:, q, :], p_st[:, q, :]).then_inc(p_stats_done, 1)

            def proj_evac(blk, par, half):
                at = proj_fill(blk, FILL_WIN + half)
                wait_filled(dve, at)
                dve.wait_ge(p_scale_steps, 8 * blk + 8)
                dst = (xp, gt)[half]
                drained(dve.scalar_tensor_tensor(out=dst[:, par, :], in0=bank[half][:, :], scalar=p_rr[:, 0:1],
                                                 in1=b_in_all[:, D * half:D * half + D],
                                                 op0=ALU.mult, op1=ALU.add), at)

            others = logit_acc.unsqueeze(2).to_broadcast([P, 2, E, E])
            own = logit[:, :, :].unsqueeze(3).to_broadcast([P, 2, E, E])
            earlier = before[:, :, :].unsqueeze(1).to_broadcast([P, 2, E, E])

            def route(blk, n):
                if n == 0:
                    dve.wait_ge(logits_copied, blk + 1)
                    for q in range(2):
                        dve.tensor_tensor(atleast[:, q], others[:, q], own[:, q], ALU.is_ge)
                        ins = dve.tensor_tensor(over[:, q], others[:, q], own[:, q], ALU.is_gt)
                else:
                    dve.wait_ge(route_steps, 8 * blk + n)
                if n == 1:
                    ins = dve.tensor_tensor(atleast, atleast, earlier, ALU.mult)
                if n == 2:
                    ins = dve.tensor_tensor(atleast, atleast, over[:, :, :, :], ALU.max)
                if n == 3:
                    ins = dve.tensor_reduce(rank, atleast, AX.X, ALU.add)
                if n == 4:
                    ins = dve.tensor_scalar(sel[:, :, :], rank, 1.5, None, ALU.is_lt)
                if n == 5:
                    ins = dve.tensor_tensor(selected, logit_acc, sel[:, :, :], ALU.mult)
                if n == 6:
                    ins = dve.tensor_reduce(top_sum[:, :], selected, AX.X, ALU.add)
                if n == 7:
                    ins = dve.scalar_tensor_tensor(out=margin, in0=logit_acc, scalar=2.0,
                                                   in1=top_sum[:, :].unsqueeze(2).to_broadcast([P, 2, E]),
                                                   op0=ALU.mult, op1=ALU.subtract)
                ins.then_inc(route_steps, 1)

            def route_gate(blk):
                dve.wait_ge(weight_ready, blk + 1)
                dve.tensor_tensor(gate[:, :, :], weight, sel[:, :, :], ALU.mult).then_inc(gate_ready, 1)

            def dec_stats(blk, q):
                wait_dec_filled(dve, blk, q)
                dve.bn_stats(d_st[:, q, :], dec_out[q][:, :]).then_inc(d_stats_done, 1)

            def dec_aggr(blk, q):
                dve.wait_ge(d_stats_done, 2 * (2 * blk + q) + 1)
                dve.sem_inc(stats_settled, 1)
                dve.bn_aggr(d_mv[:, q, :], d_st[:, q, :]).then_inc(d_stats_done, 1)

            def dec_centre(blk, q):
                v = dec_out[q][:, :]
                dve.wait_ge(d_stats_done, 2 * (2 * blk + q) + 2)
                dve.scalar_tensor_tensor(out=v, in0=v, scalar=d_mv[:, q, 0:1], in1=ln_g_all[:, :],
                                         op0=ALU.subtract, op1=ALU.mult).then_inc(d_centred, 1)

            def dec_norm(blk, q):
                t = 2 * blk + q
                dve.wait_ge(d_scale_steps, 2 * t + 2)
                if not is_first(blk):
                    dve.wait_ge(out_stored, 1 + 16 * QUAD * blk)
                dve.wait_ge(d_centred, t + 1)
                ins = dve.scalar_tensor_tensor(out=g[:, q, :], in0=dec_out[q][:, :], scalar=d_r[:, q:q + 1],
                                               in1=ln_b_all[:, :], op0=ALU.mult, op1=ALU.add)
                if q == 0:
                    drained(ins, (blk, FILL_DEC))
                else:
                    ins.then_inc(acc_drained, 1)

            def fin_y(blk):
                dve.wait_ge(t1_ready, blk + 1)
                dve.wait_ge(y_done, NQ * (blk + 1))
                dve.tensor_tensor(o, ps_y[:, :], o, ALU.add).then_inc(y_taken, 1)

            def fin_mul(blk):
                at = fin_fill(blk, FILL_FIN + 1)
                wait_filled(dve, at)
                dve.wait_ge(sg_used, sg_number(blk, 1) + 1)
                dve.tensor_tensor(g[:, 0, :], bank[1][:, :], g[:, 0, :], ALU.mult).then_inc(g_times_s, 1)
                drained(dve.tensor_tensor(g[:, 1, :], bank[1][:, :], g[:, 1, :], ALU.mult), at)

            dve.sem_inc(tile_ready, 1)
            dve.sem_inc(out_stored, 1)
            dve.memset(ones[:, :], 1.0)
            dve.memset(c_wide[:, :, :], 0.0)
            dve.memset(h[:, RING - 1, :, :], 0.0)
            dve.memset(cont_bias[M:P, :], 0.0).then_inc(consts_made, 1)
            dve.wait_ge(consts_made, 1)
            proj_stats(0)
            proj_aggr(0)
            dve.wait_ge(weights_loaded, ALL_LOADED)
            dve.wait_ge(c_summed, 1)
            for k in range(KD):
                dve.tensor_scalar(w_in[:, k, :], w_in[:, k, :], g_col[:, k:k + 1], None, ALU.mult)
            for b in range(B):
                rows = slice(SP * b, SP * b + SP)
                ins = dve.tensor_copy(c_wide[rows, :, SP - 4 + b:SP - 3 + b],
                                      ps_acc[rows, 0:F].unsqueeze(2))
            ins.then_inc(ready, 1)
            proj_evac(0, 0, 0)
            proj_evac(0, 0, 1)
            dve.wait_ge(ready, 2)

            def between(blk, par, slot):
                if slot == DVE_PROJ_STATS:
                    proj_stats(blk)
                if slot == DVE_PROJ_AGGR:
                    proj_aggr(blk)
                for half in range(2):
                    if slot == DVE_PROJ_EVAC[half]:
                        proj_evac(blk, par, half)
                for n in range(8):
                    if slot == DVE_ROUTE[n]:
                        route(blk, n)
                if slot == DVE_ROUTE_GATE:
                    route_gate(blk)
                for q in range(2):
                    if slot == DVE_DEC_STATS[q]:
                        dec_stats(blk, q)
                    if slot == DVE_DEC_AGGR[q]:
                        dec_aggr(blk, q)
                    if slot == DVE_DEC_CENTRE[q]:
                        dec_centre(blk, q)
                    if slot == DVE_DEC_NORM[q]:
                        dec_norm(blk, q)
                if slot == DVE_FIN_Y:
                    fin_y(blk)
                if slot == DVE_FIN_MUL:
                    fin_mul(blk)

            run_bodies(dve, step, between, parts=2 * F)


_PRE = "L0_attn_"
_FFN = "L0_ffn_"
_ORDER = [_PRE + n for n in ("x", "w_in", "b_in", "A", "Bm", "Cm", "Dv", "w_out", "b_out", "g_norm")] + \
         [_FFN + n for n in ("W_enc", "b_enc", "W_s2c", "b_s2c", "Wr", "br", "W1", "b1", "W2", "b2",
                             "W_c2s", "b_c2s", "W_dec", "b_dec", "ln_g", "ln_b")]
_TRANSPOSED = {_PRE + "w_in", _PRE + "A", _PRE + "Bm", _PRE + "w_out"}
_COLUMNS = {_PRE + "g_norm", _FFN + "b_enc", _FFN + "b_c2s", _FFN + "b_s2c"}


def lay_out(name, a):
    if name in _TRANSPOSED:
        a = a.T
    if name in _COLUMNS:
        a = a.reshape(-1, min(P, a.size)).T
    return np.ascontiguousarray(a)


def kernel(**inputs):
    import concourse.bacc as _bacc
    from concourse.bass_utils import run_bass_kernel_spmd as _run

    nc = _bacc.Bacc("TRN2", target_bir_lowering=False, num_devices=1)
    arrays, args = {}, []
    for name in _ORDER:
        a = lay_out(name, np.asarray(inputs[name]))
        arrays[f"in_{name}"] = a
        args.append(nc.dram_tensor(f"in_{name}", a.shape, mybir.dt.from_np(a.dtype), kind="ExternalInput").ap())
    out = nc.dram_tensor("out_0", inputs[_ORDER[0]].shape, F32, kind="ExternalOutput").ap()
    build(nc, *args, out)
    r = _run(nc, [arrays], core_ids=[0])
    return r.results[0]["out_0"]
```
